# Optimizing a Trainium2 kernel written in Bass

```python
import numpy as np
import jax
import jax.numpy as jnp

def _softmax(x, axis=-1):
    return jax.nn.softmax(x, axis=axis)

def _gelu(x):
    return jax.nn.gelu(x, approximate=True)

def _silu(x):
    return jax.nn.silu(x)

def _sigmoid(x):
    return jax.nn.sigmoid(x)

def _layernorm(x, axis=-1, eps=1e-05):
    m = jnp.mean(x, axis=axis, keepdims=True)
    v = jnp.var(x, axis=axis, keepdims=True)
    return (x - m) / jnp.sqrt(v + eps)

def _scatter_add(tgt, idx, src, axis=0):
    return tgt.at[idx].add(src)

def _segment_sum(src, seg, n):
    return jax.ops.segment_sum(src, seg, n)
kernel_name = 'mk_lm_tower_d1_tok_ids1024_r4_8096b7'

def setup_inputs(seed: int=0):
    np.random.seed(seed)
    _w = jnp.asarray

    def _rec_inputs():
        import jax
        import jax.numpy as jnp
        _rk = jax.random.key(seed)
        x = jax.random.randint(jax.random.fold_in(_rk, 1), (32, 128), 0, 64, jnp.int32)
        return x
    x = _rec_inputs()

    def _L0_tok_setup():
        import jax, jax.numpy as jnp
        import numpy as np
        B, S, E, C, H = (8, 256, 256, 64, 16)
        LN_EPS = 1e-05
        key = jax.random.key(seed)
        ks = jax.random.split(key, 12)
        sc = 0.02
        return {'input_seq': jax.random.randint(ks[0], (B, S), 0, C, dtype=jnp.int64), 'emb_W': jax.random.normal(ks[1], (E, C), jnp.float32) * sc, 'emb_b': jax.random.normal(ks[2], (E,), jnp.float32) * sc, 'Wq': jax.random.normal(ks[3], (E, E), jnp.float32) * sc, 'bq': jax.random.normal(ks[4], (E,), jnp.float32) * sc, 'Wk': jax.random.normal(ks[5], (E, E), jnp.float32) * sc, 'bk': jax.random.normal(ks[6], (E,), jnp.float32) * sc, 'Wv': jax.random.normal(ks[7], (E, E), jnp.float32) * sc, 'bv': jax.random.normal(ks[8], (E,), jnp.float32) * sc, 'Wo': jax.random.normal(ks[9], (E, E), jnp.float32) * sc, 'bo': jax.random.normal(ks[10], (E,), jnp.float32) * sc}
    _L0_tok_all = _L0_tok_setup()
    _L0_tok_in = {k: v for k, v in _L0_tok_all.items() if k in ('emb_W', 'emb_b', 'Wq', 'bq', 'Wk', 'bk', 'Wv', 'bv', 'Wo', 'bo')}
    del _L0_tok_all

    def _L0_attn_setup():
        import jax, jax.numpy as jnp
        import numpy as np
        B, S, HID, NH = (8, 1024, 256, 16)
        D = HID // NH
        LN_EPS = 1e-05

        def _l2norm(a):
            n = jnp.sqrt(jnp.sum(a * a, axis=-1, keepdims=True))
            return a / jnp.maximum(n, 1e-12)
        key = jax.random.key(seed)
        ks = jax.random.split(key, 8)
        s = 0.02
        x = jax.random.normal(ks[0], (B, S, HID), jnp.float32)
        Wq = jax.random.normal(ks[1], (HID, NH * D), jnp.float32) * s
        Wk = jax.random.normal(ks[2], (HID, NH * D), jnp.float32) * s
        Wv = jax.random.normal(ks[3], (HID, NH * D), jnp.float32) * s
        Wbeta = jax.random.normal(ks[4], (HID, NH), jnp.float32) * s
        Wg = jax.random.normal(ks[5], (HID, NH * D), jnp.float32) * s
        Wout = jax.random.normal(ks[6], (NH * D, HID), jnp.float32) * s
        ln_g = jnp.ones((NH * D,), jnp.float32)
        ln_b = jnp.zeros((NH * D,), jnp.float32)
        return {'x': x, 'Wq': Wq, 'Wk': Wk, 'Wv': Wv, 'Wbeta': Wbeta, 'Wg': Wg, 'Wout': Wout, 'ln_g': ln_g, 'ln_b': ln_b}
    _L0_attn_all = _L0_attn_setup()
    _L0_attn_in = {k: v for k, v in _L0_attn_all.items() if k in ('Wq', 'Wk', 'Wv', 'Wbeta', 'Wg', 'Wout', 'ln_g', 'ln_b')}
    del _L0_attn_all

    def _L0_ffn_setup():
        import jax, jax.numpy as jnp
        import numpy as np
        B, S, D, E, H, K = (64, 512, 256, 32, 1024, 8)
        key = jax.random.key(seed)
        k0, k1, k2, k3 = jax.random.split(key, 4)
        x = jax.random.normal(k0, (B, S, D), jnp.float32)
        gate_w = jax.random.normal(k1, (E, D), jnp.float32) * (1.0 / np.sqrt(D))
        gate_b = jnp.zeros((E,), jnp.float32)
        w1 = jax.random.normal(k2, (E, D + 1, H), jnp.float32) * (1.0 / np.sqrt(D + 1))
        w2 = jax.random.normal(k3, (E, H + 1, D), jnp.float32) * (1.0 / np.sqrt(H + 1))
        return {'x': x, 'gate_w': gate_w, 'gate_b': gate_b, 'w1': w1, 'w2': w2}
    _L0_ffn_all = _L0_ffn_setup()
    _L0_ffn_in = {k: v for k, v in _L0_ffn_all.items() if k in ('gate_w', 'gate_b', 'w1', 'w2')}
    del _L0_ffn_all
    return {'x': x, 'L0_tok_emb_W': _L0_tok_in['emb_W'], 'L0_tok_emb_b': _L0_tok_in['emb_b'], 'L0_tok_Wq': _L0_tok_in['Wq'], 'L0_tok_bq': _L0_tok_in['bq'], 'L0_tok_Wk': _L0_tok_in['Wk'], 'L0_tok_bk': _L0_tok_in['bk'], 'L0_tok_Wv': _L0_tok_in['Wv'], 'L0_tok_bv': _L0_tok_in['bv'], 'L0_tok_Wo': _L0_tok_in['Wo'], 'L0_tok_bo': _L0_tok_in['bo'], 'L0_attn_Wq': _L0_attn_in['Wq'], 'L0_attn_Wk': _L0_attn_in['Wk'], 'L0_attn_Wv': _L0_attn_in['Wv'], 'L0_attn_Wbeta': _L0_attn_in['Wbeta'], 'L0_attn_Wg': _L0_attn_in['Wg'], 'L0_attn_Wout': _L0_attn_in['Wout'], 'L0_attn_ln_g': _L0_attn_in['ln_g'], 'L0_attn_ln_b': _L0_attn_in['ln_b'], 'L0_ffn_gate_w': _L0_ffn_in['gate_w'], 'L0_ffn_gate_b': _L0_ffn_in['gate_b'], 'L0_ffn_w1': _L0_ffn_in['w1'], 'L0_ffn_w2': _L0_ffn_in['w2']}

def reference(x, L0_tok_emb_W, L0_tok_emb_b, L0_tok_Wq, L0_tok_bq, L0_tok_Wk, L0_tok_bk, L0_tok_Wv, L0_tok_bv, L0_tok_Wo, L0_tok_bo, L0_attn_Wq, L0_attn_Wk, L0_attn_Wv, L0_attn_Wbeta, L0_attn_Wg, L0_attn_Wout, L0_attn_ln_g, L0_attn_ln_b, L0_ffn_gate_w, L0_ffn_gate_b, L0_ffn_w1, L0_ffn_w2):
    import jax
    import jax.numpy as jnp

    def _L0_tok_ref(input_seq, emb_W, emb_b, Wq, bq, Wk, bk, Wv, bv, Wo, bo):
        import jax, jax.numpy as jnp
        import numpy as np
        B, S, E, C, H = (8, 256, 256, 64, 16)
        LN_EPS = 1e-05
        emb = emb_W.T[input_seq] + emb_b
        b, s, e = emb.shape
        d = e // H
        q = (emb @ Wq.T + bq).reshape(b, s, H, d)
        k = (emb @ Wk.T + bk).reshape(b, s, H, d)
        v = (emb @ Wv.T + bv).reshape(b, s, H, d)
        scores = jnp.einsum('bqhd,bkhd->bhqk', q, k) / jnp.sqrt(jnp.float32(d))
        probs = jax.nn.softmax(scores, axis=-1)
        ctx = jnp.einsum('bhqk,bkhd->bqhd', probs, v).reshape(b, s, e)
        attn_out = ctx @ Wo.T + bo
        y = attn_out + emb
        mu = jnp.mean(y, axis=(1, 2), keepdims=True)
        var = jnp.var(y, axis=(1, 2), keepdims=True)
        return (y - mu) / jnp.sqrt(var + LN_EPS)

    def _L0_attn_ref(x, Wq, Wk, Wv, Wbeta, Wg, Wout, ln_g, ln_b):
        import jax, jax.numpy as jnp
        import numpy as np
        B, S, HID, NH = (8, 1024, 256, 16)
        D = HID // NH
        LN_EPS = 1e-05

        def _l2norm(a):
            n = jnp.sqrt(jnp.sum(a * a, axis=-1, keepdims=True))
            return a / jnp.maximum(n, 1e-12)
        b, s, _ = x.shape
        nh = Wbeta.shape[1]
        d = Wq.shape[1] // nh
        q = _l2norm((x @ Wq).reshape(b, s, nh, d))
        k = _l2norm((x @ Wk).reshape(b, s, nh, d))
        v = (x @ Wv).reshape(b, s, nh, d)
        beta = jax.nn.sigmoid(x @ Wbeta)
        qT = jnp.moveaxis(q, 1, 0)
        kT = jnp.moveaxis(k, 1, 0)
        vT = jnp.moveaxis(v, 1, 0)
        bT = jnp.moveaxis(beta, 1, 0)
        state0 = jnp.zeros((b, nh, d, d), x.dtype)

        def step(state, inp):
            qt, kt, vt, bt = inp
            kk = kt[..., :, None] * kt[..., None, :]
            bb = bt[..., None, None]
            state = state * (1.0 - bb * kk) + bb * (vt[..., :, None] * kt[..., None, :])
            out_t = jnp.einsum('bhij,bhj->bhi', state, qt)
            return (state, out_t)
        _, outs = jax.lax.scan(step, state0, (qT, kT, vT, bT))
        out = jnp.moveaxis(outs, 0, 1).reshape(b, s, nh * d)
        mu = jnp.mean(out, axis=-1, keepdims=True)
        var = jnp.mean((out - mu) ** 2, axis=-1, keepdims=True)
        out = (out - mu) / jnp.sqrt(var + LN_EPS) * ln_g + ln_b
        out = out * jax.nn.silu(x @ Wg)
        return out @ Wout

    def _L0_ffn_ref(x, gate_w, gate_b, w1, w2):
        import jax, jax.numpy as jnp
        import numpy as np
        B, S, D, E, H, K = (64, 512, 256, 32, 1024, 8)
        b, s, d = x.shape
        logits = jnp.einsum('bsd,ed->bse', x, gate_w) + gate_b
        probs = jax.nn.softmax(logits, axis=-2)
        vals_t, idx_t = jax.lax.top_k(probs.transpose(0, 2, 1), K)
        vals = vals_t.transpose(0, 2, 1)
        idx = idx_t.transpose(0, 2, 1)
        flat_idx = idx.reshape(b, K * E)
        tok = jnp.take_along_axis(x, flat_idx[:, :, None], axis=1)
        tok = tok.reshape(b, K, E, d)
        merged = jnp.einsum('bked,bke->bed', tok, vals)
        ones = jnp.ones(merged.shape[:-1] + (1,), merged.dtype)
        h = jnp.einsum('bei,eih->beh', jnp.concatenate([merged, ones], -1), w1)
        h = jax.nn.gelu(h, approximate=False)
        o = jnp.einsum('bej,ejo->beo', jnp.concatenate([h, ones], -1), w2)
        out_tok = jnp.einsum('beo,bke->bkeo', o, vals).reshape(b, K * E, d)
        out = jnp.zeros_like(x).at[jnp.arange(b)[:, None], flat_idx].add(out_tok)
        return out
    h = _L0_tok_ref(x, L0_tok_emb_W, L0_tok_emb_b, L0_tok_Wq, L0_tok_bq, L0_tok_Wk, L0_tok_bk, L0_tok_Wv, L0_tok_bv, L0_tok_Wo, L0_tok_bo)
    h = h + _L0_attn_ref(_layernorm(h, axis=-1), L0_attn_Wq, L0_attn_Wk, L0_attn_Wv, L0_attn_Wbeta, L0_attn_Wg, L0_attn_Wout, L0_attn_ln_g, L0_attn_ln_b)
    h = h + _L0_ffn_ref(_layernorm(h, axis=-1), L0_ffn_gate_w, L0_ffn_gate_b, L0_ffn_w1, L0_ffn_w2)
    return h

_drawn_inputs = setup_inputs


def setup_inputs(seed=0):
    import zlib

    import numpy as np

    out = dict(_drawn_inputs(seed))
    spreads = {'L0_attn_ln_g': (1.0, 0.6), 'L0_attn_ln_b': (0.0, 0.8), 'L0_ffn_gate_b': (0.0, 2.0)}
    factors = {'L0_tok_Wq': 200.0,
     'L0_tok_bq': 200.0,
     'L0_tok_Wk': 200.0,
     'L0_tok_bk': 200.0,
     'L0_ffn_gate_w': 8.0,
     'L0_ffn_w1': 8.0,
     'L0_ffn_w2': 8.0}
    for name, (base, spread) in spreads.items():
        noise = np.random.default_rng([zlib.crc32(name.encode()), seed]).standard_normal(out[name].shape)
        drawn = base * np.exp(spread * noise) if base else spread * noise
        out[name] = jnp.asarray(drawn.astype(out[name].dtype))
    for name, factor in factors.items():
        out[name] = (out[name] * factor).astype(out[name].dtype)
    return out
```

```python
import concourse.bass as bass
from concourse import mybir
from contextlib import ExitStack

F32 = mybir.dt.float32
I32 = mybir.dt.int32
ALU = mybir.AluOpType
ACT = mybir.ActivationFunctionType
AX = mybir.AxisListType

P = 128
B, T = 32, 128
E, C = 256, 64
H, D = 16, 16
X, HID, TOPK = 32, 1024, 8
KT = E // P
PAIRS = B // 2
HP = H // 2
GB = P // H
GROUPS = B // GB
ROWS = D
RT = ROWS * T
QB = P // X
QUADS = B // QB
NPROJ = 4 * E + H
HT = HID // P
EPS = 1e-5
BIG = 1e30
START = 16


class Chain:

    def __init__(self, eng, sem):
        self.eng, self.sem, self.base, self.k, self.i, self.per, self.first = eng, sem, 0, 0, None, 0, 0

    def value(self):
        if self.i is None:
            return self.base + self.k
        return self.i * self.per + (self.base + self.k - self.first * self.per)

    def link(self, ins):
        self.k += 1
        ins.then_inc(self.sem, 1)
        self.eng.wait_ge(self.sem, self.value())

    def enter(self, i, per, first=0):
        self.base, self.k, self.i, self.per, self.first = self.base + self.k, 0, i, per, first

    def leave(self, end):
        assert self.k == self.per, (self.k, self.per)
        self.base, self.k, self.i = self.base + (end - self.first) * self.per, 0, None


def tower(nc, a, out):
    with ExitStack() as life:
        sems = {}
        fresh = []

        def sem(name):
            assert name not in sems, name
            sems[name] = life.enter_context(nc.semaphore(name))
            if "chain" not in name:
                fresh.append(sems[name])
            return sems[name]

        def sb(ctx, name, shape, dt=F32, side=None):
            return ctx.enter_context(nc.sbuf_tensor(name, shape, dt, **({"side": side} if side else {})))

        def pb(ctx, name, width):
            return ctx.enter_context(nc.psum_tensor(name, [P, width], F32))

        def start(sp):
            for s in fresh:
                sp.sem_inc(s, START)
            fresh.clear()

        m = {"start": start}
        m["rec_in"] = nc.dram_tensor("rec_in", [4, B, E, T], F32, kind="Internal").ap()
        m["rec_out"] = nc.dram_tensor("rec_out", [B, E, T], F32, kind="Internal").ap()
        m["exp_out"] = nc.dram_tensor("exp_out", [B, X, E], F32, kind="Internal").ap()
        m["ident"] = sb(life, "ident", [P, P])
        m["mhalf"] = sb(life, "mhalf", [P, PAIRS])
        tables = life.enter_context(ExitStack())
        m["h_tab"] = sb(tables, "h_tab", [P, PAIRS, E], side="right")
        m["g_tab"] = sb(tables, "g_tab", [P, PAIRS, E], side="right")
        m["onehot"] = sb(tables, "onehot", [P, PAIRS, T], side="right")
        with ExitStack() as front:
            token_attention(nc, a, m, sem, lambda n, s, d=F32: sb(front, n, s, d))
            recurrent_inputs(nc, a, m, sem, lambda n, s, d=F32: sb(front, n, s, d))
        with ExitStack() as mid:
            recurrence(nc, m, sem, lambda n, s, d=F32: sb(mid, n, s, d), lambda n, w: pb(mid, n, w))
        for name, shape in (("h2", [P, B, E]), ("picked", [P, QUADS, T]), ("merged", [P, KT, X, B]),
                            ("b1_sb", [X, HID]), ("b2_sb", [X, E])):
            m[name] = sb(life, name, shape)
        weights = life.enter_context(ExitStack())
        m["w1_sb"] = [sb(weights, "w1_sb0", [P, QB, KT, HID])]
        m["w2_sb"] = [sb(weights, "w2_sb0", [P, QB, HT, E])]
        m["ao"] = sb(tables, "ao", [P, QB, KT, T], side="right")
        m["gq"] = sb(tables, "gq", [P, 2, E], side="right")
        with ExitStack() as mid:
            def replace_tables():
                tables.close()
                m["w1_sb"].append(sb(weights, "w1_sb1", [P, QB, KT, HID], side="right"))
                m["w2_sb"].append(sb(weights, "w2_sb1", [P, QB, HT, E], side="right"))

            recurrent_outputs(nc, a, m, sem, lambda n, s, d=F32: sb(mid, n, s, d), replace_tables)
        with ExitStack() as last:
            experts(nc, a, m, sem, lambda n, s, d=F32: sb(last, n, s, d))
        weights.close()
        combine(nc, m, sem, out)


def row_statistics(nc, ch, six, mean, var, tmp):
    ch.link(nc.vector.tensor_tensor(mean, six[:, :, 1], six[:, :, 4], ALU.add))
    ch.link(nc.vector.tensor_scalar(mean, mean, 0.5, None, ALU.mult))
    ch.link(nc.vector.tensor_tensor(tmp, six[:, :, 1], mean, ALU.subtract))
    ch.link(nc.vector.tensor_tensor(tmp, tmp, tmp, ALU.mult))
    ch.link(nc.vector.tensor_tensor(var, six[:, :, 2], six[:, :, 5], ALU.add))
    ch.link(nc.vector.scalar_tensor_tensor(var, var, 1.0 / E, tmp, ALU.mult, ALU.add))


def inverse_root(nc, ch, x, y, t):
    ch.link(nc.vector.tensor_scalar(t.bitcast(I32), x.bitcast(I32), 1, None, ALU.logical_shift_right))
    ch.link(nc.vector.tensor_scalar(y.bitcast(I32), t.bitcast(I32), -1.0, float(0x5F3759DF), ALU.mult, ALU.add))
    for _ in range(3):
        ch.link(nc.vector.scalar_tensor_tensor(t, y, -0.5, y, ALU.mult, ALU.mult))
        ch.link(nc.vector.tensor_tensor(t, t, x, ALU.mult))
        ch.link(nc.vector.scalar_tensor_tensor(y, t, 1.5, y, ALU.add, ALU.mult))


def bcast_rows(vec, parts=P):
    return vec.partition_broadcast(parts)


def token_attention(nc, a, m, sem, sb):
    ident, onehot, h_tab = m["ident"], m["onehot"], m["h_tab"]
    emb_w = sb("emb_w", [P, KT, C])
    emb_bc = sb("emb_bc", [P, KT])
    w_nat = sb("w_nat", [P, 4, KT, E])
    w_t = sb("w_t", [P, 4, KT, E])
    bqk = sb("bqk", [P, 2, KT])
    bv_b, bo_b = sb("bv_b", [P, E]), sb("bo_b", [P, E])
    tok = sb("tok", [P, PAIRS, T], I32)
    cid = sb("cid", [P, 1])
    col_head = sb("col_head", [P, GB])
    row_half = sb("row_half", [P, 2])
    same_half = sb("same_half", [P, P])
    ident64 = sb("ident64", [P, C])
    cnt = sb("cnt", [P, PAIRS])
    cnt_diag = sb("cnt_diag", [P, PAIRS, C])
    cnt1 = sb("cnt1", [P, PAIRS, C])
    logc = sb("logc", [P, PAIRS, C])
    emb_t = sb("emb_t", [P, KT, P])
    q_t = sb("q_t", [P, KT, P])
    k_t = sb("k_t", [P, KT, C])
    k_heads = sb("k_heads", [P, KT, GB, C])
    v_tab = sb("v_tab", [P, E])
    v_pair = sb("v_pair", [P, HP, 2 * D + 2])
    base = sb("base", [P, E])
    score = sb("score", [P, H, C])
    stats6 = sb("stats6", [P, PAIRS, 6])
    m["cnt"], m["stats6"], m["same_half"] = cnt, stats6, same_half

    with ExitStack() as ctx:
        ps = [ctx.enter_context(nc.psum_tensor(f"s_ps{i}", [P, 512], F32)) for i in range(8)]
        block = ctx.enter_context(nc.Block())
        ld_w, ld_e, ld_x = sem("ld_w"), sem("ld_e"), sem("ld_x")
        iota_done, masks, mset = sem("iota_done"), sem("masks"), sem("mset")
        w_tp, w_cp = sem("w_tp"), sem("w_cp")
        emb_ok, q_mm, q_ok, k_ok = (sem(n) for n in ("emb_ok", "q_mm", "q_ok", "k_ok"))
        s_mm, e_tp, c_dg, c_mm, c1_ok, ln_ok = (sem(n) for n in ("s_mm", "e_tp", "c_dg", "c_mm", "c1_ok", "ln_ok"))
        vch = sem("v_chain0")

        @block.sync
        def _(sp):
            m["start"](sp)
            for n, w in enumerate(("L0_tok_Wq", "L0_tok_Wk", "L0_tok_Wv", "L0_tok_Wo")):
                sp.dma_start(w_nat[:, n], a[w].rearrange("(k p) i -> p k i", p=P)).then_inc(ld_w, 16)
            for s in range(2):
                src = a["x"].rearrange("(r s) t -> s r t", s=2)[s]
                sp.dma_start(tok[s * C:(s + 1) * C], src.partition_broadcast(C)).then_inc(ld_x, 16)

        @block.scalar
        def _(act):
            act.dma_start(emb_w[:], a["L0_tok_emb_W"].rearrange("(k p) c -> p k c", p=P)).then_inc(ld_e, 16)
            act.dma_start(emb_bc[:], a["L0_tok_emb_b"].rearrange("(k p) -> p k", p=P), allow_slow_non_contiguous=True).then_inc(ld_e, 16)
            act.dma_start(bqk[:, 0], a["L0_tok_bq"].rearrange("(k p) -> p k", p=P), allow_slow_non_contiguous=True).then_inc(ld_e, 16)
            act.dma_start(bqk[:, 1], a["L0_tok_bk"].rearrange("(k p) -> p k", p=P), allow_slow_non_contiguous=True).then_inc(ld_e, 16)
            act.dma_start(bv_b[:], bcast_rows(a["L0_tok_bv"])).then_inc(ld_e, 16)
            act.dma_start(bo_b[:], bcast_rows(a["L0_tok_bo"])).then_inc(ld_e, 16)
            for n in range(4):
                act.wait_ge(w_tp, START + n + 1)
                nc.scalar.copy(w_t[:, n], ps[n][:].rearrange("p (k o) -> p k o", k=KT)).then_inc(w_cp, 1)
            for k in range(KT):
                act.wait_ge(s_mm, START + k + 1)
                nc.scalar.copy(score[:, k * GB:(k + 1) * GB], ps[2 + k][:].rearrange("p (h c) -> p h c", c=C))
            act.wait_ge(c1_ok, START + 1)
            nc.scalar.activation(logc[:], cnt1[:], ACT.Ln).then_inc(ln_ok, 1)

        @block.gpsimd
        def _(pool):
            pch = Chain(pool, sem("p_chain0"))
            pch.link(nc.gpsimd.memset(ident[:], 0.0))
            pch.link(nc.gpsimd.affine_select(out=ident[:], in_=ident[:], compare_op=ALU.not_equal, fill=1.0,
                                             base=0, pattern=[[-1, P]], channel_multiplier=1))
            for s in range(2):
                pch.link(nc.gpsimd.iota(cid[s * C:(s + 1) * C], pattern=[[0, 1]], base=0, channel_multiplier=1,
                                        allow_small_or_imprecise_dtypes=True))
            pch.link(nc.gpsimd.memset(m["mhalf"][:], -0.5))
            for s in range(2):
                pch.link(nc.gpsimd.memset(row_half[s * C:(s + 1) * C, s:s + 1], 1.0))
                pch.link(nc.gpsimd.memset(row_half[s * C:(s + 1) * C, 1 - s:2 - s], 0.0))
            pch.link(nc.gpsimd.memset(col_head[:], 1.0))
            pch.link(nc.gpsimd.affine_select(out=col_head[:], in_=col_head[:], compare_op=ALU.is_ge, fill=0.0,
                                             base=0, pattern=[[-D, GB]], channel_multiplier=1))
            pch.link(nc.gpsimd.affine_select(out=col_head[:], in_=col_head[:], compare_op=ALU.is_ge, fill=0.0,
                                             base=D - 1, pattern=[[D, GB]], channel_multiplier=-1))
            pch.link(nc.gpsimd.memset(same_half[:], 0.0))
            for s in range(2):
                pch.link(nc.gpsimd.memset(same_half[s * C:(s + 1) * C, s * C:(s + 1) * C], 1.0))
            nc.gpsimd.tensor_tensor(ident64[:], ident[:, 0:C], ident[:, C:P], ALU.add).then_inc(masks, 1)

        @block.vector
        def _(dve):
            ch = Chain(dve, vch)
            dve.wait_ge(ld_e, START + 96)
            for k in range(KT):
                for s in range(2):
                    last = nc.vector.tensor_scalar(emb_t[:, k, s * C:(s + 1) * C], emb_w[:, k], emb_bc[:, k:k + 1],
                                                   None, ALU.add)
            last.then_inc(emb_ok, 1)
            dve.wait_ge(masks, START + 1)
            dve.wait_ge(ld_x, START + 32)
            ch.link(nc.vector.tensor_scalar(onehot[:], tok[:], cid[:, 0:1], None, ALU.is_equal))
            ch.link(nc.vector.reduce_sum(cnt[:], onehot[:], AX.X))
            nc.vector.tensor_tensor(cnt_diag[:], ident64[:].unsqueeze(1).broadcast_to([P, PAIRS, C]),
                                    cnt[:].unsqueeze(2).broadcast_to([P, PAIRS, C]), ALU.mult).then_inc(c_dg, 1)
            dve.wait_ge(q_mm, START + 1)
            for k in range(KT):
                last = nc.vector.tensor_scalar(q_t[:, k], ps[4][:, k * P:(k + 1) * P], bqk[:, 0, k:k + 1],
                                               float(D) ** -0.5, ALU.add, ALU.mult)
            last.then_inc(q_ok, 1)
            for k in range(KT):
                ch.link(nc.vector.tensor_scalar(k_t[:, k], ps[4][:, 2 * P + k * C:2 * P + (k + 1) * C],
                                                bqk[:, 1, k:k + 1], None, ALU.add))
            for k in range(KT):
                last = nc.vector.tensor_tensor(k_heads[:, k], k_t[:, k].unsqueeze(1).broadcast_to([P, GB, C]),
                                               col_head[:].unsqueeze(2).broadcast_to([P, GB, C]), ALU.mult)
            last.then_inc(k_ok, 1)
            dve.wait_ge(e_tp, START + 1)
            ch.link(nc.vector.tensor_tensor(v_tab[:], ps[5][:, 0:E], bv_b[:], ALU.add))
            half = row_half[:].unsqueeze(1)
            nc.vector.tensor_tensor(v_pair[:, :, 0:2 * D].rearrange("p g (s d) -> p g s d", d=D),
                                    v_tab[:].rearrange("p (g s d) -> p g s d", s=2, d=D),
                                    half.unsqueeze(3).broadcast_to([P, HP, 2, D]), ALU.mult)
            ch.link(nc.vector.tensor_copy(v_pair[:, :, 2 * D:], half.broadcast_to([P, HP, 2])))
            ch.link(nc.vector.tensor_tensor(base[:], ps[5][:, E:2 * E], bo_b[:], ALU.add))
            dve.wait_ge(c_mm, START + 1)
            for k in range(2):
                sl = slice(k * PAIRS // 2, (k + 1) * PAIRS // 2)
                cps = ps[6 + k][:].rearrange("p (r c) -> p r c", c=C)
                nc.vector.tensor_scalar(cnt1[:, sl], cps, 1.0, None, ALU.max)
                last = nc.vector.tensor_scalar(cnt_diag[:, sl], cps, 1.0, 0.0, ALU.subtract, ALU.min)
            last.then_inc(c1_ok, 1)
            dve.wait_ge(ln_ok, START + 1)
            ch.link(nc.vector.scalar_tensor_tensor(logc[:], cnt_diag[:], BIG, logc[:], ALU.mult, ALU.add))

        @block.tensor
        def _(pe):
            pe.wait_ge(masks, START + 1)
            for n in range(4):
                pe.wait_ge(ld_w, START + 16 * 4)
                for ki in range(KT):
                    for ko in range(KT):
                        last = nc.tensor.transpose(ps[n][:, ki * E + ko * P:ki * E + (ko + 1) * P],
                                                   w_nat[:, n, ko, ki * P:(ki + 1) * P], ident[:])
                last.then_inc(w_tp, 1)
            pe.wait_ge(emb_ok, START + 1)
            pe.wait_ge(w_cp, START + 4)
            for ko in range(KT):
                for ki in range(KT):
                    nc.tensor.matmul(ps[4][:, ko * P:(ko + 1) * P], w_t[:, 0, ki, ko * P:(ko + 1) * P], emb_t[:, ki],
                                     start=ki == 0, stop=ki == KT - 1)
            for ko in range(KT):
                for ki in range(KT):
                    last = nc.tensor.matmul(ps[4][:, 2 * P + ko * C:2 * P + (ko + 1) * C],
                                            w_t[:, 1, ki, ko * P:(ko + 1) * P], emb_t[:, ki, 0:C],
                                            start=ki == 0, stop=ki == KT - 1)
            last.then_inc(q_mm, 1)
            for ki in range(KT):
                nc.tensor.matmul(ps[5][:, 0:E], emb_t[:, ki], w_t[:, 2, ki], start=ki == 0, stop=ki == KT - 1)
            for k in range(KT):
                last = nc.tensor.transpose(ps[5][:, E + k * P:E + (k + 1) * P], emb_t[:, k], ident[:])
            last.then_inc(e_tp, 1)
            pe.wait_ge(c_dg, START + 1)
            for k in range(2):
                last = nc.tensor.matmul(ps[6 + k][:], same_half[:],
                                        cnt_diag[:, k * PAIRS // 2:(k + 1) * PAIRS // 2].rearrange("p r c -> p (r c)"),
                                        start=True, stop=True)
            last.then_inc(c_mm, 1)
            pe.wait_ge(q_ok, START + 1)
            pe.wait_ge(k_ok, START + 1)
            for k in range(KT):
                nc.tensor.matmul(ps[2 + k][:], q_t[:, k], k_heads[:, k].rearrange("p h c -> p (h c)"),
                                 start=True, stop=True).then_inc(s_mm, 1)

    with ExitStack() as ctx:
        def sbx(n, s):
            return ctx.enter_context(nc.sbuf_tensor(n, s, F32))
        logit = [sbx(f"logit{i}", [P, H, C]) for i in range(2)]
        prob = [sbx(f"prob{i}", [P, H * C]) for i in range(2)]
        prob_t = [sbx(f"prob_t{i}", [P, HP, P]) for i in range(2)]
        top = [sbx(f"top{i}", [P, H]) for i in range(2)]
        rden = [sbx(f"rden{i}", [P, HP, 2]) for i in range(2)]
        cx = [sbx(f"cx{i}", [P, E]) for i in range(2)]
        cx_t = [sbx(f"cx_t{i}", [P, KT, P]) for i in range(2)]
        bn = [sbx(f"bn{i}", [P, 6]) for i in range(2)]
        yrow = [sbx(f"yrow{i}", [P, E]) for i in range(2)]
        ps_t = [ctx.enter_context(nc.psum_tensor(f"ps_t{i}", [P, HP * P], F32)) for i in range(2)]
        ps_c = [ctx.enter_context(nc.psum_tensor(f"ps_c{i}", [P, 512], F32)) for i in range(2)]
        ps_y = [ctx.enter_context(nc.psum_tensor(f"ps_y{i}", [P, 512], F32)) for i in range(2)]
        block = ctx.enter_context(nc.Block())

        def par(name):
            return [sem(f"{name}{i}") for i in range(2)]
        lg_ok, ex_ok, pt_mm, pt_ok, cx_mm, cx_ok, ct_mm, ct_ok, y_mm, y_ok = (
            par(n) for n in ("lg_ok", "ex_ok", "pt_mm", "pt_ok", "cx_mm", "cx_ok", "ct_mm", "ct_ok", "y_mm", "y_ok"))
        sc_ok = par("sc_ok")
        TURNS = PAIRS // 2

        @block.sync
        def _(sp):
            m["start"](sp)

        @block.gpsimd
        def _(pool):
            with nc.gpsimd.Fori(0, TURNS) as i:
                for s in range(2):
                    pool.wait_ge(ex_ok[s], START + i)
                    nc.gpsimd.tensor_tensor(logit[s][:], score[:],
                                            logc[:, bass.ds(2 * i + s, 1)].broadcast_to([P, H, C]), ALU.add)\
                        .then_inc(sc_ok[s], 1)

        @block.vector
        def _(dve):
            ch = Chain(dve, sem("v_chain1"))

            def softmax_input(i, s):
                dve.wait_ge(sc_ok[s], START + i + 1)
                ch.link(nc.vector.reduce_max(top[s][:], logit[s][:], AX.X))
                nc.vector.tensor_tensor(logit[s][:], logit[s][:], top[s][:].unsqueeze(2).broadcast_to([P, H, C]),
                                        ALU.subtract).then_inc(lg_ok[s], 1)

            def finish(i, s):
                dve.wait_ge(cx_mm[s], START + i + 1)
                c = ps_c[s][:, 0:HP * (2 * D + 2)].rearrange("p (g n) -> p g n", g=HP)
                ch.link(nc.vector.reciprocal(rden[s][:], c[:, :, 2 * D:]))
                nc.vector.tensor_tensor(cx[s][:].rearrange("p (g s d) -> p g s d", s=2, d=D),
                                        c[:, :, 0:2 * D].rearrange("p g (s d) -> p g s d", d=D),
                                        rden[s][:].unsqueeze(3).broadcast_to([P, HP, 2, D]),
                                        ALU.mult).then_inc(cx_ok[s], 1)

            def output(i, s, r):
                dve.wait_ge(y_mm[s], START + i + 1)
                ch.link(nc.vector.tensor_tensor(yrow[s][:], ps_y[s][:, E:2 * E], base[:], ALU.add))
                ch.link(nc.vector.bn_stats(bn[s][:], yrow[s][:]))
                nc.vector.tensor_copy(stats6[:, bass.ds(r, 1)], bn[s][:].unsqueeze(1))
                nc.vector.tensor_copy(h_tab[:, bass.ds(r, 1)], yrow[s][:].unsqueeze(1)).then_inc(y_ok[s], 1)

            def step(t, new=True, old=True):
                for s in range(2):
                    if new:
                        softmax_input(t, s)
                    if old:
                        finish(t - 1, s)
                if old:
                    for s in range(2):
                        output(t - 1, s, 2 * (t - 1) + s)

            step(0, old=False)
            with nc.vector.Fori(1, TURNS) as t:
                ch.enter(t, 2 * 4, 1)
                step(t)
            ch.leave(TURNS)
            step(TURNS, new=False)

        @block.scalar
        def _(act):
            def exponential(i, s):
                act.wait_ge(lg_ok[s], START + i + 1)
                act.wait_ge(pt_mm[s], START + i)
                nc.scalar.activation(prob[s][:], logit[s][:].rearrange("p h c -> p (h c)"),
                                     ACT.Exp).then_inc(ex_ok[s], 1)

            def copy_prob(i, s):
                act.wait_ge(pt_mm[s], START + i + 1)
                act.wait_ge(cx_mm[s], START + i)
                nc.scalar.copy(prob_t[s][:].rearrange("p g c -> p (g c)"), ps_t[s][:]).then_inc(pt_ok[s], 1)

            def copy_context(i, s):
                act.wait_ge(ct_mm[s], START + i + 1)
                act.wait_ge(y_mm[s], START + i)
                nc.scalar.copy(cx_t[s][:].rearrange("p k c -> p (k c)"), ps_y[s][:, 0:E]).then_inc(ct_ok[s], 1)

            def step(t, new=True, old=True):
                if new:
                    for s in range(2):
                        exponential(t, s)
                        copy_prob(t, s)
                if old:
                    for s in range(2):
                        copy_context(t - 1, s)

            step(0, old=False)
            with nc.scalar.Fori(1, TURNS) as t:
                step(t)
            step(TURNS, new=False)

        @block.tensor
        def _(pe):
            def transpose_prob(i, s):
                pe.wait_ge(ex_ok[s], START + i + 1)
                pe.wait_ge(pt_ok[s], START + i)
                for g in range(HP):
                    last = nc.tensor.transpose(ps_t[s][:, g * P:(g + 1) * P], prob[s][:, g * P:(g + 1) * P], ident[:])
                last.then_inc(pt_mm[s], 1)

            def context(i, s):
                pe.wait_ge(pt_ok[s], START + i + 1)
                pe.wait_ge(cx_ok[s], START + i)
                n = 2 * D + 2
                for g in range(HP):
                    last = nc.tensor.matmul(ps_c[s][:, g * n:(g + 1) * n], prob_t[s][:, g], v_pair[:, g],
                                            start=True, stop=True)
                last.then_inc(cx_mm[s], 1)

            def transpose_context(i, s):
                pe.wait_ge(cx_ok[s], START + i + 1)
                pe.wait_ge(y_ok[s], START + i)
                for k in range(KT):
                    last = nc.tensor.transpose(ps_y[s][:, k * P:(k + 1) * P], cx[s][:, k * P:(k + 1) * P], ident[:])
                last.then_inc(ct_mm[s], 1)

            def project(i, s):
                pe.wait_ge(ct_ok[s], START + i + 1)
                for k in range(KT):
                    last = nc.tensor.matmul(ps_y[s][:, E:2 * E], cx_t[s][:, k], w_t[:, 3, k],
                                            start=k == 0, stop=k == KT - 1)
                last.then_inc(y_mm[s], 1)

            def step(t, new=True, old=True):
                for s in range(2):
                    if old:
                        context(t - 1, s)
                    if new:
                        transpose_prob(t, s)
                if old:
                    for s in range(2):
                        transpose_context(t - 1, s)
                    for s in range(2):
                        project(t - 1, s)

            step(0, old=False)
            with nc.tensor.Fori(1, TURNS) as t:
                step(t)
            step(TURNS, new=False)


def recurrent_inputs(nc, a, m, sem, sb):
    ident, onehot, h_tab, g_tab, mhalf = m["ident"], m["onehot"], m["h_tab"], m["g_tab"], m["mhalf"]
    cnt, stats6, same_half, rec_in = m["cnt"], m["stats6"], m["same_half"], m["rec_in"]
    w_all = sb("w_all", [P, KT, NPROJ])
    wn = sb("wn", [P, PAIRS])
    wm = sb("wm", [P, 2, PAIRS])
    dm = sb("dm", [P, PAIRS])
    mean_row, var_row = sb("mean_row", [P, PAIRS]), sb("var_row", [P, PAIRS])
    ex2 = sb("ex2", [P, PAIRS])
    mean_b = sb("mean_b", [P, PAIRS])
    varb = sb("varb", [P, PAIRS])
    rstd_b = sb("rstd_b", [P, PAIRS])
    mean_1 = sb("mean_1", [P, PAIRS])
    var1 = sb("var1", [P, PAIRS])
    rstd_1 = sb("rstd_1", [P, PAIRS])

    with ExitStack() as ctx:
        ps = ctx.enter_context(nc.psum_tensor("st_ps", [P, 2, 512], F32))
        block = ctx.enter_context(nc.Block())
        ld_a, w_ok, sum_mm, pow_in, pow_ok = (sem(n) for n in ("ld_a", "w_ok", "sum_mm", "pow_in", "pow_ok"))

        @block.sync
        def _(sp):
            m["start"](sp)
            for n, w in enumerate(("L0_attn_Wq", "L0_attn_Wk", "L0_attn_Wv", "L0_attn_Wg")):
                sp.dma_start(w_all[:, :, n * E:(n + 1) * E], a[w].rearrange("(k p) o -> p k o", p=P)).then_inc(ld_a, 16)
            sp.dma_start(w_all[:, :, 4 * E:], a["L0_attn_Wbeta"].rearrange("(k p) o -> p k o", p=P)).then_inc(ld_a, 16)
            sp.wait_ge(ld_a, START + 16 * 5)

        @block.vector
        def _(dve):
            ch = Chain(dve, sem("v_chain2"))
            mean_r, var_r = mean_row[:], var_row[:]
            row_statistics(nc, ch, stats6[:], mean_r, var_r, dm[:])
            ch.link(nc.vector.tensor_scalar(wn[:], cnt[:], 1.0 / T, None, ALU.mult))
            nc.vector.tensor_tensor(wm[:, 0], wn[:], mean_r, ALU.mult).then_inc(w_ok, 1)
            dve.wait_ge(sum_mm, START + 1)
            ch.link(nc.vector.tensor_copy(mean_b[:], ps[:, 0, 0:PAIRS]))
            ch.link(nc.vector.tensor_tensor(dm[:], mean_r, mean_b[:], ALU.subtract))
            ch.link(nc.vector.tensor_tensor(ex2[:], dm[:], dm[:], ALU.mult))
            ch.link(nc.vector.tensor_tensor(ex2[:], ex2[:], var_r, ALU.add))
            nc.vector.tensor_tensor(wm[:, 1], wn[:], ex2[:], ALU.mult).then_inc(w_ok, 1)
            dve.wait_ge(sum_mm, START + 2)
            nc.vector.tensor_scalar(varb[:], ps[:, 1, 0:PAIRS], EPS, None, ALU.add).then_inc(pow_in, 1)
            dve.wait_ge(pow_ok, START + 1)
            ch.link(nc.vector.tensor_tensor(mean_1[:], dm[:], rstd_b[:], ALU.mult))
            ch.link(nc.vector.tensor_tensor(var1[:], var_r, rstd_b[:], ALU.mult))
            ch.link(nc.vector.tensor_tensor(var1[:], var1[:], rstd_b[:], ALU.mult))
            nc.vector.tensor_scalar(var1[:], var1[:], EPS, None, ALU.add).then_inc(pow_in, 1)

        @block.gpsimd
        def _(pool):
            pool.wait_ge(pow_in, START + 1)
            nc.gpsimd.tensor_tensor(rstd_b[:], varb[:], mhalf[:, 0:PAIRS], ALU.pow).then_inc(pow_ok, 1)
            pool.wait_ge(pow_in, START + 2)
            nc.gpsimd.tensor_tensor(rstd_1[:], var1[:], mhalf[:, 0:PAIRS], ALU.pow).then_inc(pow_ok, 1)

        @block.tensor
        def _(pe):
            for n in range(2):
                pe.wait_ge(w_ok, START + n + 1)
                nc.tensor.matmul(ps[:, n, 0:PAIRS], same_half[:], wm[:, n], start=True, stop=True).then_inc(sum_mm, 1)

    with ExitStack() as ctx:
        def sbx(n, s):
            return ctx.enter_context(nc.sbuf_tensor(n, s, F32))
        x1 = [sbx(f"x1_{i}", [P, E]) for i in range(2)]
        x1_t = [sbx(f"x1_t{i}", [P, KT, P]) for i in range(2)]
        sq = [sbx(f"sq{i}", [P, 2 * H, D]) for i in range(2)]
        norm2 = [sbx(f"norm2_{i}", [P, 2 * H]) for i in range(2)]
        newton = [sbx(f"newton{i}", [P, 2 * H]) for i in range(2)]
        rnorm = [sbx(f"rnorm{i}", [P, 2 * H]) for i in range(2)]
        beta = [sbx(f"beta{i}", [P, H]) for i in range(2)]
        sig = [sbx(f"sig{i}", [P, E]) for i in range(2)]
        tab = [sbx(f"tab{i}", [P, 4, E]) for i in range(2)]
        hot = [sbx(f"hot{i}", [P, T]) for i in range(2)]
        feat = [sbx(f"feat{i}", [P, 2, 4, KT, T]) for i in range(2)]
        ps_x = [ctx.enter_context(nc.psum_tensor(f"ps_x{i}", [P, 512], F32)) for i in range(2)]
        ps_qk = ctx.enter_context(nc.psum_tensor("ps_qk", [P, 2 * E], F32))
        ps_vg = ctx.enter_context(nc.psum_tensor("ps_vg", [P, 2 * E], F32))
        ps_f = ctx.enter_context(nc.psum_tensor("ps_f", [P, 2, 4, KT, T], F32))
        block = ctx.enter_context(nc.Block())

        def par(name):
            return [sem(f"{name}{i}") for i in range(2)]
        x_ok, xt_mm, xt_ok, pj_mm, sq_ok, sg_ok, tb_ok, hot_ok, f_mm, f_ok, f_st = (
            par(n) for n in ("x_ok", "xt_mm", "xt_ok", "pj_mm", "sq_ok", "sg_ok", "tb_ok", "hot_ok",
                             "f_mm", "f_ok", "f_st"))
        vg_free = par("vg_free")
        TURNS = PAIRS // 2

        @block.vector
        def _(dve):
            ch = Chain(dve, sem("v_chain3"))

            def rows(i, s, r):
                h = h_tab[:, bass.ds(r, 1)]
                ch.link(nc.vector.tensor_scalar(h, h, mean_b[:, bass.ds(r, 1)], rstd_b[:, bass.ds(r, 1)],
                                                ALU.subtract, ALU.mult))
                dve.wait_ge(xt_mm[s], START + i)
                nc.vector.tensor_scalar(x1[s][:].unsqueeze(1), h, mean_1[:, bass.ds(r, 1)], rstd_1[:, bass.ds(r, 1)],
                                        ALU.subtract, ALU.mult).then_inc(x_ok[s], 1)

            def norms(i, s):
                dve.wait_ge(sq_ok[s], START + i + 1)
                ch.link(nc.vector.reduce_sum(norm2[s][:], sq[s][:], AX.X))
                ch.link(nc.vector.tensor_scalar(norm2[s][:], norm2[s][:], 1e-24, None, ALU.max))
                inverse_root(nc, ch, norm2[s][:], rnorm[s][:], newton[s][:])

            def table(i, s, r):
                dve.wait_ge(sg_ok[s], START + i + 1)
                dve.wait_ge(f_mm[s], START + i)
                bb = beta[s][:].unsqueeze(2).broadcast_to([P, H, D])
                nc.vector.tensor_tensor(tab[s][:, 3].rearrange("p (h d) -> p h d", d=D),
                                        ps_vg[:, 0:E].rearrange("p (h d) -> p h d", d=D), bb, ALU.mult)
                nc.vector.tensor_tensor(g_tab[:, bass.ds(r, 1)], ps_vg[:, E:].unsqueeze(1), sig[s][:].unsqueeze(1), ALU.mult)\
                    .then_inc(vg_free[s], 1)
                ch.link(nc.vector.tensor_tensor(tab[s][:, 0:2].rearrange("p j (h d) -> p (j h) d", d=D),
                                                ps_qk[:].rearrange("p (h d) -> p h d", d=D),
                                                rnorm[s][:].unsqueeze(2).broadcast_to([P, 2 * H, D]), ALU.mult))
                nc.vector.tensor_tensor(tab[s][:, 2].rearrange("p (h d) -> p h d", d=D),
                                        tab[s][:, 1].rearrange("p (h d) -> p h d", d=D), bb, ALU.mult)\
                    .then_inc(tb_ok[s], 1)

            def step(t, new=True, old=True):
                for s in range(2):
                    if new:
                        rows(t, s, 2 * t + s)
                for s in range(2):
                    if old:
                        norms(t - 1, s)
                        table(t - 1, s, 2 * (t - 1) + s)

            step(0, old=False)
            with nc.vector.Fori(1, TURNS) as t:
                ch.enter(t, 2 * (1 + 13 + 1), 1)
                step(t)
            ch.leave(TURNS)
            step(TURNS, new=False)

        @block.gpsimd
        def _(pool):
            with nc.gpsimd.Fori(0, TURNS) as i:
                for s in range(2):
                    pool.wait_ge(f_mm[s], START + i)
                    nc.gpsimd.tensor_copy(hot[s][:].unsqueeze(1), onehot[:, bass.ds(2 * i + s, 1)]).then_inc(hot_ok[s], 1)

        @block.scalar
        def _(act):
            def copy_rows(i, s):
                act.wait_ge(xt_mm[s], START + i + 1)
                act.wait_ge(pj_mm[s], START + i)
                nc.scalar.copy(x1_t[s][:].rearrange("p k c -> p (k c)"), ps_x[s][:, 0:E]).then_inc(xt_ok[s], 1)

            def squares(i, s):
                act.wait_ge(pj_mm[s], START + i + 1)
                act.wait_ge(tb_ok[s], START + i)
                nc.scalar.square(sq[s][:], ps_qk[:].rearrange("p (h d) -> p h d", d=D)).then_inc(sq_ok[s], 1)
                nc.scalar.activation(beta[s][:], ps_x[s][:, E:E + H], ACT.Sigmoid)
                nc.scalar.activation(sig[s][:], ps_vg[:, E:], ACT.Sigmoid).then_inc(sg_ok[s], 1)

            def copy_features(i, s):
                act.wait_ge(f_mm[s], START + i + 1)
                act.wait_ge(f_st[s], START + 128 * i)
                for q in range(2):
                    ins = nc.scalar.copy(feat[s][:, q], ps_f[:, q])
                ins.then_inc(f_ok[s], 1)

            def step(t, new=True, old=True, older=True):
                if old:
                    squares(t - 1, 0)
                if older:
                    copy_features(t - 2, 1)
                if new:
                    copy_rows(t, 0)
                if old:
                    squares(t - 1, 1)
                    copy_features(t - 1, 0)
                if new:
                    copy_rows(t, 1)

            step(0, old=False, older=False)
            step(1, older=False)
            with nc.scalar.Fori(2, TURNS) as t:
                step(t)
            step(TURNS, new=False)
            step(TURNS + 1, new=False, old=False)

        @block.tensor
        def _(pe):
            def transpose_rows(i, s):
                pe.wait_ge(x_ok[s], START + i + 1)
                pe.wait_ge(sg_ok[s], START + i)
                for k in range(KT):
                    last = nc.tensor.transpose(ps_x[s][:, k * P:(k + 1) * P], x1[s][:, k * P:(k + 1) * P], ident[:])
                last.then_inc(xt_mm[s], 1)

            def project(i, s):
                pe.wait_ge(xt_ok[s], START + i + 1)
                pe.wait_ge(tb_ok[1 - s], START + i + s)
                pe.wait_ge(vg_free[1 - s], START + i + s)
                for dst, lo, n in ((ps_qk[:], 0, 2 * E), (ps_vg[:], 2 * E, 2 * E), (ps_x[s][:, E:E + H], 4 * E, H)):
                    for k in range(KT):
                        last = nc.tensor.matmul(dst, x1_t[s][:, k], w_all[:, k, lo:lo + n],
                                                start=k == 0, stop=k == KT - 1)
                last.then_inc(pj_mm[s], 1)

            def to_positions(i, s):
                pe.wait_ge(tb_ok[s], START + i + 1)
                pe.wait_ge(hot_ok[s], START + i + 1)
                pe.wait_ge(f_ok[1 - s], START + i + s)
                for j in range(4):
                    for k in range(KT):
                        for q in range(2):
                            rows = slice(q * C, (q + 1) * C)
                            last = nc.tensor.matmul(ps_f[:, q, j, k], tab[s][rows, j, k * P:(k + 1) * P],
                                                    hot[s][rows], start=True, stop=True)
                last.then_inc(f_mm[s], 1)

            def step(t, new=True, old=True, older=True):
                if old:
                    project(t - 1, 0)
                if older:
                    to_positions(t - 2, 1)
                if new:
                    transpose_rows(t, 0)
                if old:
                    project(t - 1, 1)
                    to_positions(t - 1, 0)
                if new:
                    transpose_rows(t, 1)

            step(0, old=False, older=False)
            step(1, older=False)
            with nc.tensor.Fori(2, TURNS) as t:
                step(t)
            step(TURNS, new=False)
            step(TURNS + 1, new=False, old=False)

        @block.sync
        def _(sp):
            m["start"](sp)
            dst = rec_in.rearrange("j b (k p) t -> j b p k t", p=P)
            with nc.sync.Fori(0, TURNS) as i:
                for s in range(2):
                    sp.wait_ge(f_ok[s], START + i + 1)
                    for q in range(2):
                        for j in range(4):
                            sp.dma_start(dst[j][bass.ds(4 * i + 2 * s + q, 1)].rearrange("b p k t -> (b p) k t"),
                                         feat[s][:, q, j]).then_inc(f_st[s], 16)
            for s in range(2):
                sp.wait_ge(f_st[s], START + 128 * TURNS)


def recurrence(nc, m, sem, sb, pb):
    ident, rec_in, rec_out = m["ident"], m["rec_in"], m["rec_out"]
    inp = sb("inp", [P, 2, 4, RT])
    upd = [sb(f"upd{i}", [P, RT]) for i in range(2)]
    state = sb("state", [P, RT])
    read = [sb(f"read{i}", [P, RT]) for i in range(2)]
    prod = sb("prod", [P, RT])
    osb = sb("osb", [P, RT])
    ps_a = pb("ps_a", RT)
    ps_o = pb("ps_o", RT)

    chunks = [(0, False)] + [c for d in range(1, D // 2) for c in ((d, False), (d, True))] + [(D // 2, False)]
    N = len(chunks)

    def shift(c):
        d, mirrored = chunks[c]
        return D - d if mirrored else d

    def pieces(s):
        return [(0, D - s, s)] + ([(D - s, D, s - D)] if s else [])

    with ExitStack() as ctx:
        block = ctx.enter_context(nc.Block())
        ld_g = sem("ld_g")
        upd_ok, upd_free, prod_ok, fac_ok, read_ok, read_free, o_ok, o_st = (
            sem(n) for n in ("upd_ok", "upd_free", "prod_ok", "fac_ok", "read_ok", "read_free", "rec_ok", "rec_st"))
        a_zero = sem("a_zero")
        src = rec_in.rearrange("j (g b) (h i) t -> g (b h) j (i t)", b=GB, h=H)
        NF = D // 2 + 1

        def part(par, j, lo, hi):
            return inp[:, bass.ds(par, 1), j, lo * T:hi * T].rearrange("p o n -> p (o n)")

        @block.sync
        def _(sp):
            m["start"](sp)
            for j in range(4):
                sp.dma_start(inp[:, 0, j], src[0][:, j]).then_inc(ld_g, 16)
            with nc.sync.Fori(1, GROUPS) as g:
                sp.wait_ge(ld_g, START + 64 * g)
                sp.wait_ge(read_ok, START + (g - 1) * N)
                sp.wait_ge(upd_ok, START + (g - 1) * N)
                for j in range(4):
                    sp.dma_start(inp[:, bass.ds(g % 2, 1), j], src[bass.ds(g, 1), :, j].rearrange("g p n -> p g n"))\
                        .then_inc(ld_g, 16)
                sp.wait_ge(o_ok, START + g)
                sp.dma_start(rec_out.rearrange("(g b) (h i) t -> g (b h) (i t)", b=GB, h=H)[bass.ds(g - 1, 1)]
                             .rearrange("g p n -> (g p) n"), osb[:]).then_inc(o_st, 16)
            sp.wait_ge(o_ok, START + GROUPS)
            sp.dma_start(rec_out.rearrange("(g b) (h i) t -> g (b h) (i t)", b=GB, h=H)[GROUPS - 1], osb[:])\
                .then_inc(o_st, 16)
            sp.wait_ge(o_st, START + 16 * GROUPS)

        @block.gpsimd
        def _(pool):
            with nc.gpsimd.Fori(0, GROUPS) as g:
                pool.wait_ge(ld_g, START + g * 64 + 64)
                for c in range(N):
                    pool.wait_ge(upd_free, START + g * N + c + 1)
                    for lo, hi, off in pieces(shift(c)):
                        last = nc.gpsimd.tensor_tensor(upd[c % 2][:, lo * T:hi * T], part(g % 2, 3, lo, hi),
                                                       part(g % 2, 1, lo + off, hi + off), ALU.mult)
                    last.then_inc(upd_ok, 1)

        @block.scalar
        def _(act):
            def copy_out(g):
                act.wait_ge(read_free, START + g * N + N + 2)
                act.wait_ge(o_st, START + g * 16)
                nc.scalar.copy(osb[:], ps_o[:]).then_inc(o_ok, 1)

            act.wait_ge(a_zero, START + 1)
            def factors(g, which):
                for f in which:
                    act.wait_ge(prod_ok, START + g * NF + f + 1)
                    act.wait_ge(upd_free, START + g * N + sum(d < f for d, _ in chunks) + 2)
                    rows = D if f < D // 2 else D // 2
                    nc.scalar.activation(ps_a[:, 0:rows * T].rearrange("p (i t) -> p i t", t=T)[:, :, 1:],
                                         prod[:, 0:rows * T].rearrange("p (i t) -> p i t", t=T)[:, :, 1:],
                                         ACT.Copy, bias=1.0, scale=-1.0).then_inc(fac_ok, 1)

            factors(0, range(NF))
            with nc.scalar.Fori(1, GROUPS) as g:
                factors(g, [0])
                copy_out(g - 1)
                factors(g, range(1, NF))
            copy_out(GROUPS - 1)

        @block.vector
        def _(dve):
            ch = Chain(dve, sem("v_chain4"))
            ch.link(nc.vector.memset(ps_a[:].rearrange("p (i t) -> p i t", t=T)[:, :, 0], 0.0))
            dve.sem_inc(upd_free, 2)
            dve.sem_inc(a_zero, 1)

            def products(g, f):
                if f:
                    dve.wait_ge(fac_ok, START + g * NF + f)
                rows = D if f < D // 2 else D // 2
                for lo, hi, off in pieces(f):
                    if lo < rows:
                        last = nc.vector.tensor_tensor(prod[:, lo * T:hi * T], part(g % 2, 2, lo, hi),
                                                       part(g % 2, 1, lo + off, hi + off), ALU.mult)
                last.then_inc(prod_ok, 1)

            with nc.vector.Fori(0, GROUPS) as g:
                dve.wait_ge(ld_g, START + g * 64 + 64)
                products(g, 0)
                for c, (d, mirrored) in enumerate(chunks):
                    last_use = c == N - 1 or chunks[c + 1][0] != d
                    if last_use and d < D // 2:
                        products(g, d + 1)
                    if not mirrored:
                        dve.wait_ge(fac_ok, START + g * NF + d + 1)
                    dve.wait_ge(upd_ok, START + g * N + c + 1)
                    dve.wait_ge(read_ok, START + g * N + c)
                    if mirrored:
                        runs = [(d, D, 0), (0, d, D - d)]
                    elif d == D // 2:
                        runs = [(0, d, 0), (d, D, 0)]
                    else:
                        runs = [(0, D, 0)]
                    for lo, hi, f0 in runs:
                        ins = nc.vector.tensor_tensor_scan(state[:, lo * T:hi * T],
                                                           ps_a[:, f0 * T:(f0 + hi - lo) * T],
                                                           upd[c % 2][:, lo * T:hi * T], 0.0, ALU.mult, ALU.add)
                    ins.then_inc(upd_free, 1)
                    dve.wait_ge(upd_free, START + g * N + c + 3)
                    dve.wait_ge(read_free, START + g * N + c + 1)
                    for lo, hi, off in pieces(shift(c)):
                        ins = nc.vector.tensor_tensor(read[c % 2][:, lo * T:hi * T], state[:, lo * T:hi * T],
                                                      part(g % 2, 0, lo + off, hi + off), ALU.mult)
                    ins.then_inc(read_ok, 1)

        @block.tensor
        def _(pe):
            pe.sem_inc(read_free, 2)
            with nc.tensor.Fori(0, GROUPS) as g:
                pe.wait_ge(o_ok, START + g)
                for c in range(N):
                    pe.wait_ge(read_ok, START + g * N + c + 1)
                    for n in range(4):
                        last = nc.tensor.matmul(ps_o[:, n * 512:(n + 1) * 512], ident[:],
                                                read[c % 2][:, n * 512:(n + 1) * 512],
                                                start=c == 0, stop=c == N - 1)
                    last.then_inc(read_free, 1)


def recurrent_outputs(nc, a, m, sem, sb, replace_tables):
    ident, onehot, h_tab, g_tab, mhalf = m["ident"], m["onehot"], m["h_tab"], m["g_tab"], m["mhalf"]
    h2, picked, merged, rec_out = m["h2"], m["picked"], m["merged"], m["rec_out"]
    w_out = sb("w_out", [P, KT, E])
    lng, lnb = sb("lng", [P, E]), sb("lnb", [P, E])
    gw = sb("gw", [X, E])
    gw_t = sb("gw_t", [P, KT, X])
    gb = sb("gb", [P, 1])
    hot = sb("hot_q", [P, QB, T])
    hq = sb("hq", [P, 2, E])
    ao, gq = m["ao"], m["gq"]
    bn = sb("bn_q", [P, QB, 6])
    mean = sb("mean_q", [P, 2, QB])
    tmp = sb("tmp_q", [P, QB])
    idle = sb("idle", [P, TOPK])
    ve = sb("ve_q", [P, 2, QB])
    rs = sb("rs_q", [P, 2, QB])
    z = sb("z_q", [P, QB, E])
    z_t = sb("z_t", [P, QB, KT, P])
    x2 = sb("x2", [P, QB, E])
    x2_t = sb("x2_t", [P, QB, KT, P])
    lg = sb("lg_q", [P, T])
    nmx = sb("nmx", [P, 1])
    den = sb("den", [P, 1])
    rden = sb("rden_q", [P, 1])
    pr = sb("pr", [P, T])
    top8 = sb("top8", [P, TOPK])
    rep = sb("rep", [P, T])
    mask = sb("mask", [P, T])
    pm = sb("pm", [P, T])
    pm_t = sb("pm_t", [P, P])

    with ExitStack() as ctx:
        ps_a = ctx.enter_context(nc.psum_tensor("pq_a", [P, QB, E], F32))
        ps_g = ctx.enter_context(nc.psum_tensor("pq_g", [P, QB, E], F32))
        ps_z = ctx.enter_context(nc.psum_tensor("pq_z", [P, QB, E], F32))
        ps_h = ctx.enter_context(nc.psum_tensor("pq_h", [P, QB, E], F32))
        names = ("o_ld", "o_w", "o_gwt", "o_gwt_ok", "o_hot", "o_at", "o_gt", "o_zn", "o_z", "o_zt",
                 "o_ztok", "o_h", "o_hc", "o_x", "o_xt", "o_xtok", "o_lg", "o_nm", "o_ex", "o_pm", "o_pt", "o_ptok",
                 "o_mm", "o_mc", "o_pmc", "o_zs")
        (o_ld, o_w, o_gwt, o_gwt_ok, o_hot, o_at, o_gt, o_zn, o_z, o_zt, o_ztok, o_h, o_hc, o_x, o_xt,
         o_xtok, o_lg, o_nm, o_ex, o_pm, o_pt, o_ptok, o_mm, o_mc, o_pmc, o_zs) = (sem(n) for n in names)
        w1_ld, w2_ld = ([[sem(f"{n}{s}{h}") for h in range(2)] for s in range(2)] for n in ("w1_ld", "w2_ld"))
        wbias, hot_zero = sem("wbias"), sem("hot_zero")
        o_bn, o_pow = ([sem(f"{n}{k}") for k in range(2)] for n in ("o_bn", "o_pow"))
        m["w1_ld"], m["w2_ld"], m["wbias"] = w1_ld, w2_ld, wbias

        pch, ch = Chain(nc.gpsimd, sem("p_chain1")), Chain(nc.vector, sem("v_chain5"))

        def sync_program(sp, tail):
            m["start"](sp)
            if tail:
                for h in range(2):
                    load_w1(sp, a, QB, h, m["w1_sb"][1], w1_ld[1])
                for h in range(2):
                    load_w2(sp, a, QB, h, m["w2_sb"][1], w2_ld[1])
                return
            src = rec_out.rearrange("b (k p) t -> p b k t", p=P)
            with nc.sync.Fori(0, QUADS) as i:
                sp.wait_ge(o_at, START + i)
                for j in range(QB):
                    sp.dma_start(ao[:, j], src[:, bass.ds(QB * i + j, 1)].rearrange("p b k t -> p (b k) t"))\
                        .then_inc(o_ld, 16)

        def scalar_head(act):
            act.dma_start(w_out[:], a["L0_attn_Wout"].rearrange("(k p) o -> p k o", p=P)).then_inc(o_w, 16)
            act.dma_start(lng[:], bcast_rows(a["L0_attn_ln_g"])).then_inc(o_w, 16)
            act.dma_start(lnb[:], bcast_rows(a["L0_attn_ln_b"])).then_inc(o_w, 16)
            act.dma_start(gw[:], a["L0_ffn_gate_w"]).then_inc(o_w, 16)
            for j in range(QB):
                act.dma_start(gb[j * X:(j + 1) * X], a["L0_ffn_gate_b"].unsqueeze(1)).then_inc(o_w, 16)
            load_bias(act, a, m, wbias)
            for h in range(2):
                load_w1(act, a, 0, h, m["w1_sb"][0], w1_ld[0])
            for h in range(2):
                load_w2(act, a, 0, h, m["w2_sb"][0], w2_ld[0])
            act.wait_ge(o_gwt, START + 1)
            nc.scalar.copy(gw_t[:], ps_z[:, 0, 0:KT * X].rearrange("p (k x) -> p k x", k=KT)).then_inc(o_gwt_ok, 1)
            act.wait_ge(hot_zero, START + 1)

        def scalar_program(act, tail):
            def copy_x2(i):
                act.wait_ge(o_xt, START + i + 1)
                nc.scalar.copy(x2_t[:].rearrange("p j k c -> p (j k c)"), ps_z[:].rearrange("p j e -> p (j e)"))\
                    .then_inc(o_xtok, 1)

            def exponential(i):
                act.wait_ge(o_nm, START + i + 1)
                nc.scalar.activation(pr[:], lg[:], ACT.Exp, bias=nmx[:, 0:1], scale=1.0, accum_out=den[:, 0:1])\
                    .then_inc(o_ex, 1)

            def copy_picks(i):
                act.wait_ge(o_pt, START + i + 1)
                nc.scalar.copy(pm_t[:], ps_g[:, 1, 0:P]).then_inc(o_ptok, 1)

            def copy_merged(i):
                act.wait_ge(o_mm, START + i + 1)
                for k in range(KT):
                    ins = nc.scalar.copy(merged[:, k, :, bass.ds(QB * i, QB)],
                                         ps_g[:, 2, k * P:(k + 1) * P].rearrange("p (j x) -> p x j", j=QB))
                ins.then_inc(o_mc, 1)

            def copy_z(i):
                act.wait_ge(o_zt, START + i + 1)
                nc.scalar.copy(z_t[:].rearrange("p j k c -> p (j k c)"), ps_z[:].rearrange("p j e -> p (j e)"))\
                    .then_inc(o_ztok, 1)

            def copy_h2(i):
                act.wait_ge(o_h, START + i + 1)
                nc.scalar.copy(h2[:, bass.ds(QB * i, QB)], ps_h[:]).then_inc(o_hc, 1)

            def entries(i):
                act.wait_ge(o_h, START + i)
                for s in range(2):
                    rows = slice(s * C, (s + 1) * C)
                    nc.scalar.copy(hot[rows, s::2], onehot[rows, bass.ds(2 * i, 2)])
                nc.scalar.copy(gq[:], g_tab[:, bass.ds(2 * i, 2)]).then_inc(o_hot, 1)
                nc.scalar.copy(hq[:], h_tab[:, bass.ds(2 * i, 2)]).then_inc(o_hot, 1)

            def step(t, new=True, old=True, older=True):
                if older:
                    copy_x2(t - 2)
                if old:
                    copy_z(t - 1)
                if older:
                    exponential(t - 2)
                if old:
                    copy_h2(t - 1)
                if older:
                    copy_picks(t - 2)
                if new:
                    entries(t)
                if older:
                    copy_merged(t - 2)

            if tail:
                step(QUADS, new=False)
                step(QUADS + 1, new=False, old=False)
                return
            scalar_head(act)
            step(0, old=False, older=False)
            step(1, older=False)
            with nc.scalar.Fori(2, QUADS) as t:
                step(t)

        def gpsimd_program(pool, tail):

            def root(n, i):
                pool.wait_ge(o_bn[n], START + i + 1)
                nc.gpsimd.tensor_tensor(rs[:, n], ve[:, n], mhalf[:, 0:QB], ALU.pow).then_inc(o_pow[n], 1)

            def scale(i):
                pool.wait_ge(o_zn, START + i + 1)
                pch.link(nc.gpsimd.tensor_tensor(z[:], z[:], lng[:].unsqueeze(1).broadcast_to([P, QB, E]), ALU.mult))
                nc.gpsimd.tensor_tensor(z[:], z[:], lnb[:].unsqueeze(1).broadcast_to([P, QB, E]), ALU.add)\
                    .then_inc(o_zs, 1)

            def keep_picks(i):
                pool.wait_ge(o_pm, START + i + 1)
                nc.gpsimd.tensor_copy(picked[:, bass.ds(i, 1)], pm[:].unsqueeze(1)).then_inc(o_pmc, 1)

            def step(t, new=True, old=True, older=True):
                if new:
                    root(0, t)
                    scale(t)
                if old:
                    root(1, t - 1)
                if older:
                    keep_picks(t - 2)

            if tail:
                step(QUADS, new=False)
                step(QUADS + 1, new=False, old=False)
                return
            nc.gpsimd.memset(hot[:], 0.0).then_inc(hot_zero, 1)
            step(0, old=False, older=False)
            step(1, older=False)
            with nc.gpsimd.Fori(2, QUADS) as t:
                pch.enter(t, 1, 2)
                step(t)
            pch.leave(QUADS)

        def vector_program(dve, tail):
            def statistics(src, n):
                for j in range(QB):
                    last = nc.vector.bn_stats(bn[:, j], src[:, j])
                ch.link(last)
                row_statistics(nc, ch, bn[:], mean[:, n], ve[:, n], tmp[:])
                nc.vector.tensor_scalar(ve[:, n], ve[:, n], EPS, None, ALU.add).then_inc(o_bn[n], 1)

            def normalise(i):
                dve.wait_ge(o_at, START + i + 1)
                statistics(ps_a, 0)
                dve.wait_ge(o_pow[0], START + i + 1)
                dve.wait_ge(o_zt, START + i)
                for j in range(QB):
                    last = nc.vector.tensor_scalar(z[:, j], ps_a[:, j], mean[:, 0, j:j + 1], rs[:, 0, j:j + 1],
                                                   ALU.subtract, ALU.mult)
                last.then_inc(o_zn, 1)

            def gate(i):
                dve.wait_ge(o_gt, START + i + 1)
                dve.wait_ge(o_zs, START + i + 1)
                nc.vector.tensor_tensor(z[:], z[:], ps_g[:], ALU.mult).then_inc(o_z, 1)

            def normalise_h2(i):
                dve.wait_ge(o_hc, START + i + 1)
                statistics(ps_h, 1)
                dve.wait_ge(o_pow[1], START + i + 1)
                dve.wait_ge(o_mm, START + i)
                for j in range(QB):
                    last = nc.vector.tensor_scalar(x2[:, j], ps_h[:, j], mean[:, 1, j:j + 1], rs[:, 1, j:j + 1],
                                                   ALU.subtract, ALU.mult)
                last.then_inc(o_x, 1)

            def pick(i):
                dve.wait_ge(o_lg, START + i + 1)
                ch.link(nc.vector.tensor_scalar(lg[:], ps_g[:, 0, 0:T], gb[:, 0:1], None, ALU.add))
                nc.vector.tensor_reduce(nmx[:], lg[:], AX.X, ALU.max, negate=True).then_inc(o_nm, 1)
                dve.wait_ge(o_ex, START + i + 1)
                ch.link(nc.vector.reciprocal(rden[:], den[:]))
                ch.link(nc.vector.tensor_scalar(pr[:], pr[:], rden[:, 0:1], None, ALU.mult))
                nc.vector.tensor_copy(idle[:, 0:1], rden[:])
                ch.link(nc.vector.max(top8[:], pr[:]))
                nc.vector.tensor_copy(idle[:], top8[:])
                ch.link(nc.vector.match_replace(rep[:], top8[:], pr[:], -1.0))
                ch.link(nc.vector.tensor_tensor(mask[:], rep[:], pr[:], ALU.not_equal))
                dve.wait_ge(o_pt, START + i)
                dve.wait_ge(o_pmc, START + i)
                nc.vector.tensor_tensor(pm[:], pr[:], mask[:], ALU.mult).then_inc(o_pm, 1)

            def step(t, new=True, old=True, older=True):
                if old:
                    gate(t - 1)
                if new:
                    normalise(t)
                if older:
                    pick(t - 2)
                if old:
                    normalise_h2(t - 1)

            if tail:
                step(QUADS, new=False)
                step(QUADS + 1, new=False, old=False)
                return
            dve.wait_ge(o_w, START + 16 * 8)
            step(0, old=False, older=False)
            step(1, older=False)
            with nc.vector.Fori(2, QUADS) as t:
                ch.enter(t, 2 * (1 + 6) + 6, 2)
                step(t)
            ch.leave(QUADS)

        def tensor_head(pe):
            pe.wait_ge(o_w, START + 16 * 8)
            for k in range(KT):
                last = nc.tensor.transpose(ps_z[:, 0, k * X:(k + 1) * X], gw[:, k * P:(k + 1) * P], ident[0:X, 0:X])
            last.then_inc(o_gwt, 1)
            pe.wait_ge(o_gwt_ok, START + 1)

        def tensor_program(pe, tail):
            def transpose_in(i):
                pe.wait_ge(o_ld, START + 64 * i + 64)
                pe.wait_ge(o_zn, START + i)
                for j in range(QB):
                    for k in range(KT):
                        last = nc.tensor.transpose(ps_a[:, j, k * P:(k + 1) * P], ao[:, j, k], ident[:])
                last.then_inc(o_at, 1)

            def gates(i, older):
                pe.wait_ge(o_hot, START + 2 * i + 1)
                pe.wait_ge(o_z, START + i)
                pe.wait_ge(o_mc, START + older)
                for j in range(QB):
                    last = nc.tensor.matmul(ps_g[:, j], hot[:, j], gq[:, j // 2], start=True, stop=True)
                last.then_inc(o_gt, 1)

            def transpose_z(i, older):
                pe.wait_ge(o_z, START + i + 1)
                pe.wait_ge(o_xtok, START + older)
                for j in range(QB):
                    for k in range(KT):
                        last = nc.tensor.transpose(ps_z[:, j, k * P:(k + 1) * P], z[:, j, k * P:(k + 1) * P], ident[:])
                last.then_inc(o_zt, 1)

            def residual_and_project(i):
                pe.wait_ge(o_ztok, START + i + 1)
                pe.wait_ge(o_hot, START + 2 * i + 2)
                pe.wait_ge(o_x, START + i)
                for j in range(QB):
                    nc.tensor.matmul(ps_h[:, j], hot[:, j], hq[:, j // 2], start=True, stop=False)
                    for k in range(KT):
                        last = nc.tensor.matmul(ps_h[:, j], z_t[:, j, k], w_out[:, k], start=False, stop=k == KT - 1)
                last.then_inc(o_h, 1)

            def transpose_x2(i):
                pe.wait_ge(o_x, START + i + 1)
                pe.wait_ge(o_ztok, START + i + 1)
                for j in range(QB):
                    for k in range(KT):
                        last = nc.tensor.transpose(ps_z[:, j, k * P:(k + 1) * P], x2[:, j, k * P:(k + 1) * P], ident[:])
                last.then_inc(o_xt, 1)

            def logits(i):
                pe.wait_ge(o_xtok, START + i + 1)
                for j in range(QB):
                    for k in range(KT):
                        last = nc.tensor.matmul(ps_g[j * X:(j + 1) * X, 0, 0:T], gw_t[:, k], x2_t[:, j, k],
                                                start=k == 0, stop=k == KT - 1)
                last.then_inc(o_lg, 1)

            def merge(i):
                pe.wait_ge(o_pm, START + i + 1)
                nc.tensor.transpose(ps_g[:, 1, 0:P], pm[:], ident[:]).then_inc(o_pt, 1)
                pe.wait_ge(o_ptok, START + i + 1)
                for j in range(QB):
                    for k in range(KT):
                        last = nc.tensor.matmul(ps_g[:, 2, k * P + j * X:k * P + (j + 1) * X],
                                                x2[:, j].rearrange("t (p k) -> t k p", k=KT)[:, k],
                                                pm_t[:, j * X:(j + 1) * X], start=True, stop=True)
                last.then_inc(o_mm, 1)

            def step(t, new=True, old=True, older=True):
                if older:
                    transpose_x2(t - 2)
                if new:
                    transpose_in(t)
                if old:
                    transpose_z(t - 1, t - 1 if older else 0)
                if older:
                    logits(t - 2)
                if old:
                    residual_and_project(t - 1)
                if older:
                    merge(t - 2)
                if new:
                    gates(t, t - 1 if older else 0)

            if tail:
                step(QUADS, new=False)
                step(QUADS + 1, new=False, old=False)
                return
            tensor_head(pe)
            step(0, old=False, older=False)
            step(1, older=False)
            with nc.tensor.Fori(2, QUADS) as t:
                step(t)

        for tail in (False, True):
            if tail:
                replace_tables()
            with nc.Block() as block:
                @block.sync
                def _(sp):
                    sync_program(sp, tail)

                @block.scalar
                def _(act):
                    scalar_program(act, tail)

                @block.gpsimd
                def _(pool):
                    gpsimd_program(pool, tail)

                @block.vector
                def _(dve):
                    vector_program(dve, tail)

                @block.tensor
                def _(pe):
                    tensor_program(pe, tail)


def load_bias(eng, a, m, done):
    eng.dma_start(m["b1_sb"][:], a["L0_ffn_w1"][:, E]).then_inc(done, 16)
    eng.dma_start(m["b2_sb"][:], a["L0_ffn_w2"][:, HID]).then_inc(done, 16)


def load_w1(eng, a, x, h, dst, done):
    eng.dma_start(dst[:, :, h],
                  a["L0_ffn_w1"][bass.ds(x, QB), 0:E].rearrange("x (p k) n -> k p x n", k=KT)[h]).then_inc(done[h], 16)


def load_w2(eng, a, x, h, dst, done):
    half = slice(h * HT // 2, (h + 1) * HT // 2)
    eng.dma_start(dst[:, :, half].rearrange("p x n e -> p x (n e)"),
                  a["L0_ffn_w2"][bass.ds(x, QB), 0:HID].rearrange("x (p h n) e -> h p x (n e)", h=2, n=HT // 2)[h])\
        .then_inc(done[h], 16)


def experts(nc, a, m, sem, sb):
    ident, merged, exp_out = m["ident"], m["merged"], m["exp_out"]
    w1, w2, b1, b2, w1_ld, w2_ld = m["w1_sb"], m["w2_sb"], m["b1_sb"], m["b2_sb"], m["w1_ld"], m["w2_ld"]
    mq = sb("mq", [P, KT, QB, B])
    sel = sb("sel", [X, QB, B])
    hg = sb("hg", [P, HID])
    h_t = sb("h_t", [P, HT, P])
    eo = sb("eo", [P, X // QB, E])

    with ExitStack() as ctx:
        ps_1 = [ctx.enter_context(nc.psum_tensor(f"ps_1{s}", [P, HID], F32)) for s in range(2)]
        ps_t = ctx.enter_context(nc.psum_tensor("ps_ht", [P, HT, P], F32))
        ps_2 = [ctx.enter_context(nc.psum_tensor(f"ps_2{s}", [P, 512], F32)) for s in range(2)]
        block = ctx.enter_context(nc.Block())
        mq_ok, gl, ht, htok, eo_ok, eo_st = (
            sem(n) for n in ("mq_ok", "gl", "ht", "htok", "eo_ok", "eo_st"))
        l1, l2 = ([sem(f"{n}{s}") for s in range(2)] for n in ("l1_", "l2_"))
        TURNS = X // QB // 2


        @block.gpsimd
        def _(pool):
            with nc.gpsimd.Fori(0, TURNS) as i:
                for s in range(2):
                    q = 2 * i + s
                    pool.wait_ge(l2[1 - s], START + 2 * i + 2 * s)
                    nc.gpsimd.tensor_copy(mq[:], merged[:, :, bass.ds(QB * q, QB)])
                    nc.gpsimd.tensor_copy(sel[:], ident[0:X, bass.ds(QB * q, QB)].unsqueeze(2)
                                          .broadcast_to([X, QB, B])).then_inc(mq_ok, 1)

        @block.scalar
        def _(act):
            with nc.scalar.Fori(0, TURNS) as i:
                for s in range(2):
                    act.wait_ge(l1[s], START + 2 * i + 2)
                    act.wait_ge(ht, START + 4 * i + 2 * s)
                    nc.scalar.activation(hg[:], ps_1[s][:], ACT.Gelu).then_inc(gl, 1)

        @block.sync
        def _(sp):
            m["start"](sp)

            def store(q):
                sp.wait_ge(eo_ok, START + q + 1)
                for j in range(QB):
                    sp.dma_start(exp_out[:, bass.ds(QB * q + j, 1)].rearrange("b x e -> b (x e)"),
                                 eo[j * B:(j + 1) * B, bass.ds(q, 1)].rearrange("b i e -> b (i e)")).then_inc(eo_st, 16)

            with nc.sync.Fori(1, TURNS) as i:
                for s in range(2):
                    for h in range(2):
                        sp.wait_ge(l1[s], START + 2 * i - 1 + h)
                        load_w1(sp, a, QB * (2 * i + s), h, w1[s], w1_ld[s])
                    for h in range(2):
                        sp.wait_ge(l2[s], START + 2 * i - 1 + h)
                        load_w2(sp, a, QB * (2 * i + s), h, w2[s], w2_ld[s])
                    store(2 * (i - 1) + s)
            for s in range(2):
                store(2 * (TURNS - 1) + s)
            sp.wait_ge(eo_st, START + 16 * QB * TURNS * 2)

        @block.vector
        def _(dve):
            with nc.vector.Fori(0, TURNS) as i:
                for s in range(2):
                    dve.wait_ge(l2[1 - s], START + 2 * i + 2 * s)
                    for h in range(2):
                        dve.wait_ge(ht, START + 4 * i + 2 * s + h + 1)
                        half = slice(h * HT // 2, (h + 1) * HT // 2)
                        nc.vector.tensor_copy(h_t[:, half], ps_t[:, half]).then_inc(htok, 1)
                    dve.wait_ge(l2[s], START + 2 * i + 2)
                    nc.vector.tensor_copy(eo[:, bass.ds(2 * i + s, 1)], ps_2[s][:, 0:E].unsqueeze(1)).then_inc(eo_ok, 1)

        @block.tensor
        def _(pe):
            def first_layer(i, s):
                pe.wait_ge(mq_ok, START + 2 * i + s + 1)
                pe.wait_ge(gl, START + 2 * i + s - 1)
                for n in range(2):
                    cols = slice(n * 512, (n + 1) * 512)
                    nc.tensor.matmul(ps_1[s][:, cols], sel[:].rearrange("x j b -> x (j b)"), b1[:, cols],
                                     start=True, stop=False, skip_group_check=True)
                for k in range(KT):
                    pe.wait_ge(w1_ld[s][k], START + 16 * i + 16)
                    for n in range(2):
                        cols = slice(n * 512, (n + 1) * 512)
                        for j in range(QB):
                            last = nc.tensor.matmul(ps_1[s][j * B:(j + 1) * B, cols], mq[:, k, j],
                                                    w1[s][:, j, k, cols], start=False, stop=k == KT - 1,
                                                    skip_group_check=True)
                    last.then_inc(l1[s], 1)

            def transpose_hidden(i, s):
                pe.wait_ge(gl, START + 2 * i + s + 1)
                pe.wait_ge(htok, START + 4 * i + 2 * s)
                for h in range(2):
                    for n in range(h * HT // 2, (h + 1) * HT // 2):
                        last = nc.tensor.transpose(ps_t[:, n], hg[:].rearrange("q (p n) -> q n p", n=HT)[:, n], ident[:])
                    last.then_inc(ht, 1)

            def second_layer(i, s):
                pe.wait_ge(eo_ok, START + 2 * i + s)
                nc.tensor.matmul(ps_2[s][:, 0:E], sel[:].rearrange("x j b -> x (j b)"), b2[:],
                                 start=True, stop=False, skip_group_check=True)
                for n in range(HT):
                    if n % (HT // 2) == 0:
                        pe.wait_ge(w2_ld[s][n // (HT // 2)], START + 16 * i + 16)
                        pe.wait_ge(htok, START + 4 * i + 2 * s + n // (HT // 2) + 1)
                    for j in range(QB):
                        last = nc.tensor.matmul(ps_2[s][j * B:(j + 1) * B, 0:E], h_t[:, n, j * B:(j + 1) * B],
                                                w2[s][:, j, n], start=False, stop=n == HT - 1, skip_group_check=True)
                    if n % (HT // 2) == HT // 2 - 1:
                        last.then_inc(l2[s], 1)

            pe.wait_ge(m["wbias"], START + 32)
            with nc.tensor.Fori(0, TURNS) as i:
                for s in range(2):
                    first_layer(i, s)
                    transpose_hidden(i, s)
                    second_layer(i, s)


def combine(nc, m, sem, out):
    h2, picked, exp_out = m["h2"], m["picked"], m["exp_out"]
    with ExitStack() as ctx:
        def sbx(n, s):
            return ctx.enter_context(nc.sbuf_tensor(n, s, F32))
        oq = sbx("oq", [P, QUADS, E])
        res = [sbx(f"res{s}", [P, QB, E]) for s in range(2)]
        ps_o = [ctx.enter_context(nc.psum_tensor(f"ps_fo{j}", [P, 512], F32)) for j in range(QB)]
        ps_o2 = [ctx.enter_context(nc.psum_tensor(f"ps_go{j}", [P, 512], F32)) for j in range(QB)]
        psx = [ps_o, ps_o2]
        block = ctx.enter_context(nc.Block())

        def par(name):
            return [sem(f"{name}{i}") for i in range(2)]
        f_mm, f_add, f_out = (par(n) for n in ("z_mm", "z_add", "z_out"))
        f_ld = sem("z_ld")
        TURNS = QUADS // 2

        @block.sync
        def _(sp):
            m["start"](sp)
            src = exp_out.rearrange("(q j) x e -> (j x) q e", j=QB)
            for h in range(2):
                quads = slice(h * QUADS // 2, (h + 1) * QUADS // 2)
                sp.dma_start(oq[:, quads], src[:, quads]).then_inc(f_ld, 16)
                sp.wait_ge(f_ld, START + 16 * (h + 1))

        @block.tensor
        def _(pe):
            for q in range(QUADS):
                i, s = divmod(q, 2)
                if q % (QUADS // 2) == 0:
                    pe.wait_ge(f_ld, START + (32 if q else 16))
                pe.wait_ge(f_add[s], START + i)
                for j in range(QB):
                    rows = slice(j * X, (j + 1) * X)
                    last = nc.tensor.matmul(psx[s][j][:, 0:E], picked[rows, q], oq[rows, q], start=True, stop=True)
                last.then_inc(f_mm[s], 1)

        @block.vector
        def _(dve):
            with nc.vector.Fori(0, TURNS) as i:
                for s in range(2):
                    dve.wait_ge(f_mm[s], START + i + 1)
                    dve.wait_ge(f_out[s], START + 16 * i)
                    for j in range(QB):
                        last = nc.vector.tensor_tensor(res[s][:, bass.ds(j, 1)], psx[s][j][:, 0:E].unsqueeze(1),
                                                       h2[:, bass.ds(2 * QB * i + QB * s + j, 1)], ALU.add)
                    last.then_inc(f_add[s], 1)

        @block.scalar
        def _(act):
            dst = out.rearrange("(q j) t e -> q t j e", j=QB)
            with nc.scalar.Fori(0, TURNS) as i:
                for s in range(2):
                    act.wait_ge(f_add[s], START + i + 1)
                    act.dma_start(dst[bass.ds(2 * i + s, 1)].rearrange("q t j e -> (q t) j e"), res[s][:])\
                        .then_inc(f_out[s], 16)
            for s in range(2):
                act.wait_ge(f_out[s], START + 16 * TURNS)


_INS = ["x", "L0_tok_emb_W", "L0_tok_emb_b", "L0_tok_Wq", "L0_tok_bq", "L0_tok_Wk", "L0_tok_bk", "L0_tok_Wv",
        "L0_tok_bv", "L0_tok_Wo", "L0_tok_bo", "L0_attn_Wq", "L0_attn_Wk", "L0_attn_Wv", "L0_attn_Wbeta",
        "L0_attn_Wg", "L0_attn_Wout", "L0_attn_ln_g", "L0_attn_ln_b", "L0_ffn_gate_w", "L0_ffn_gate_b",
        "L0_ffn_w1", "L0_ffn_w2"]


def kernel(**inputs):
    import numpy as _np
    import concourse.bacc as _bacc
    from concourse import mybir as _mybir
    from concourse.bass_utils import run_bass_kernel_spmd as _run

    nc = _bacc.Bacc("TRN2", target_bir_lowering=False, num_devices=1)
    arrays, args = {}, {}
    for name in _INS:
        v = _np.ascontiguousarray(inputs[name])
        arrays[f"in_{name}"] = v
        args[name] = nc.dram_tensor(f"in_{name}", v.shape, _mybir.dt.from_np(v.dtype), kind="ExternalInput").ap()
    out = nc.dram_tensor("out_dram", (B, T, E), _mybir.dt.float32, kind="ExternalOutput").ap()
    tower(nc, args, out)
    r = _run(nc, [arrays], core_ids=[0])
    return r.results[0]["out_dram"]
```

```python
import concourse.bass as bass
from concourse import mybir
from contextlib import ExitStack

F32 = mybir.dt.float32
I32 = mybir.dt.int32
ALU = mybir.AluOpType
ACT = mybir.ActivationFunctionType
AX = mybir.AxisListType

P = 128
B, T = 32, 128
E, C = 256, 64
H, D = 16, 16
X, HID, TOPK = 32, 1024, 8
KT = E // P
PAIRS = B // 2
HP = H // 2
GB = P // H
GROUPS = B // GB
ROWS = D
RT = ROWS * T
QB = P // X
QUADS = B // QB
NPROJ = 4 * E + H
HT = HID // P
EPS = 1e-5
BIG = 1e30
START = 16


class Chain:

    def __init__(self, eng, sem):
        self.eng, self.sem, self.base, self.k, self.i, self.per, self.first = eng, sem, 0, 0, None, 0, 0

    def value(self):
        if self.i is None:
            return self.base + self.k
        return self.i * self.per + (self.base + self.k - self.first * self.per)

    def link(self, ins):
        self.k += 1
        ins.then_inc(self.sem, 1)
        self.eng.wait_ge(self.sem, self.value())

    def enter(self, i, per, first=0):
        self.base, self.k, self.i, self.per, self.first = self.base + self.k, 0, i, per, first

    def leave(self, end):
        assert self.k == self.per, (self.k, self.per)
        self.base, self.k, self.i = self.base + (end - self.first) * self.per, 0, None


def tower(nc, a, out):
    with ExitStack() as life:
        sems = {}
        fresh = []

        def sem(name):
            assert name not in sems, name
            sems[name] = life.enter_context(nc.semaphore(name))
            if "chain" not in name:
                fresh.append(sems[name])
            return sems[name]

        def sb(ctx, name, shape, dt=F32, side=None):
            return ctx.enter_context(nc.sbuf_tensor(name, shape, dt, **({"side": side} if side else {})))

        def pb(ctx, name, width):
            return ctx.enter_context(nc.psum_tensor(name, [P, width], F32))

        def start(sp):
            for s in fresh:
                sp.sem_inc(s, START)
            fresh.clear()

        m = {"start": start}
        m["rec_in"] = nc.dram_tensor("rec_in", [B, 4, E, T], F32, kind="Internal").ap()
        m["rec_out"] = nc.dram_tensor("rec_out", [B, E, T], F32, kind="Internal").ap()
        m["exp_out"] = nc.dram_tensor("exp_out", [B, X, E], F32, kind="Internal").ap()
        m["ident"] = sb(life, "ident", [P, P])
        m["mhalf"] = sb(life, "mhalf", [P, PAIRS])
        for name, shape in (("w_out", [P, KT, E]), ("lng", [P, E]), ("lnb", [P, E]), ("gw", [X, E]), ("gb", [P, 1])):
            m[name] = sb(life, name, shape)
        tables = life.enter_context(ExitStack())
        m["h_tab"] = sb(tables, "h_tab", [P, PAIRS, E], side="right")
        m["g_tab"] = sb(tables, "g_tab", [P, PAIRS, E], side="right")
        m["onehot"] = sb(tables, "onehot", [P, PAIRS, T], side="right")
        m["ao"] = sb(tables, "ao", [P, QB, KT, T], side="right")
        m["gq"] = sb(tables, "gq", [P, 2, E], side="right")
        m["osb"] = sb(tables, "osb", [P, RT], side="right")
        for name, shape in (("cnt", [P, PAIRS]), ("stats6", [P, PAIRS, 6]), ("same_half", [P, P])):
            m[name] = sb(tables, name, shape, side="right")
        with ExitStack() as front:
            token_attention(nc, a, m, sem, lambda n, s, d=F32: sb(front, n, s, d))
        held = life.enter_context(ExitStack())
        m["inp"] = sb(held, "inp", [P, 2, 4, RT])
        m["feat"] = [sb(held, f"feat{i}", [P, 2, 4, KT, T]) for i in range(2)]
        m["upd"] = [sb(held, f"upd{i}", [P, RT]) for i in range(2)]
        m["prod"] = sb(held, "prod", [P, RT])
        with ExitStack() as front:
            recurrent_inputs(nc, a, m, sem, lambda n, s, d=F32: sb(front, n, s, d))
        with ExitStack() as mid:
            recurrence(nc, a, m, sem, lambda n, s, d=F32: sb(mid, n, s, d), lambda n, w: pb(mid, n, w))
        held.close()
        for name, shape in (("h2", [P, B, E]), ("picked", [P, QUADS, T]), ("merged", [P, KT, X, B]),
                            ("b1_sb", [X, HID]), ("b2_sb", [X, E])):
            m[name] = sb(life, name, shape)
        weights = life.enter_context(ExitStack())
        m["w1_sb"] = [sb(weights, "w1_sb0", [P, QB, KT, HID])]
        m["w2_sb"] = [sb(weights, "w2_sb0", [P, QB, HT, E])]
        with ExitStack() as mid:
            def replace_tables():
                tables.close()
                m["w1_sb"].append(sb(weights, "w1_sb1", [P, QB, KT, HID], side="right"))
                m["w2_sb"].append(sb(weights, "w2_sb1", [P, QB, HT, E], side="right"))

            recurrent_outputs(nc, a, m, sem, lambda n, s, d=F32: sb(mid, n, s, d), replace_tables)
        with ExitStack() as last:
            experts(nc, a, m, sem, lambda n, s, d=F32: sb(last, n, s, d))
        weights.close()
        combine(nc, m, sem, out)


def row_statistics(nc, ch, six, mean, var, tmp, eps):
    nc.vector.tensor_tensor(tmp, six[:, :, 1], six[:, :, 4], ALU.subtract)
    nc.vector.tensor_tensor(mean, six[:, :, 1], six[:, :, 4], ALU.add)
    ch.link(nc.vector.tensor_tensor(var, six[:, :, 2], six[:, :, 5], ALU.add))
    nc.vector.scalar_tensor_tensor(tmp, tmp, 0.25, tmp, ALU.mult, ALU.mult)
    nc.vector.tensor_scalar(mean, mean, 0.5, None, ALU.mult)
    ch.link(nc.vector.tensor_scalar(var, var, 1.0 / E, eps, ALU.mult, ALU.add))
    return nc.vector.tensor_tensor(var, var, tmp, ALU.add)


def inverse_root(nc, ch, x, y, t):
    ch.link(nc.vector.tensor_scalar(t.bitcast(I32), x.bitcast(I32), 1, None, ALU.logical_shift_right))
    ch.link(nc.vector.tensor_scalar(y.bitcast(I32), t.bitcast(I32), -1.0, float(0x5F3759DF), ALU.mult, ALU.add))
    for _ in range(3):
        ch.link(nc.vector.scalar_tensor_tensor(t, y, -0.5, y, ALU.mult, ALU.mult))
        ch.link(nc.vector.tensor_tensor(t, t, x, ALU.mult))
        ch.link(nc.vector.scalar_tensor_tensor(y, t, 1.5, y, ALU.add, ALU.mult))


def bcast_rows(vec, parts=P):
    return vec.partition_broadcast(parts)


def token_attention(nc, a, m, sem, sb):
    ident, onehot, h_tab = m["ident"], m["onehot"], m["h_tab"]
    emb_w = sb("emb_w", [P, KT, C])
    emb_bc = sb("emb_bc", [P, KT])
    w_nat = sb("w_nat", [P, 4, KT, E])
    w_t = sb("w_t", [P, 4, KT, E])
    bqk = sb("bqk", [P, 2, KT])
    bv_b, bo_b = sb("bv_b", [P, E]), sb("bo_b", [P, E])
    tok = sb("tok", [P, PAIRS, T], I32)
    cid = sb("cid", [P, 1])
    col_head = sb("col_head", [P, GB])
    row_half = sb("row_half", [P, 2])
    ident64 = sb("ident64", [P, C])
    cnt, stats6, same_half = m["cnt"], m["stats6"], m["same_half"]
    cnt1, absent = sb("cnt1", [P, PAIRS]), sb("absent", [P, PAIRS])
    log_diag = sb("log_diag", [P, PAIRS, C])
    logc = sb("logc", [P, PAIRS, C])
    emb_t = sb("emb_t", [P, KT, P])
    q_t = sb("q_t", [P, KT, P])
    k_t = sb("k_t", [P, KT, C])
    k_heads = sb("k_heads", [P, KT, GB, C])
    v_tab = sb("v_tab", [P, E])
    v_pair = sb("v_pair", [P, HP, 2 * D + 2])
    base = sb("base", [P, E])
    score = sb("score", [P, H, C])

    with ExitStack() as ctx:
        ps = [ctx.enter_context(nc.psum_tensor(f"s_ps{i}", [P, 512], F32)) for i in range(8)]
        block = ctx.enter_context(nc.Block())
        ld_w, ld_e, ld_x = sem("ld_w"), sem("ld_e"), sem("ld_x")
        masks = sem("masks")
        w_tp, w_cp = sem("w_tp"), sem("w_cp")
        emb_ok, q_mm, q_ok, k_ok = (sem(n) for n in ("emb_ok", "q_mm", "q_ok", "k_ok"))
        s_mm, e_tp, c_dg, c_mm, c1_ok, ln_ok = (sem(n) for n in ("s_mm", "e_tp", "c_dg", "c_mm", "c1_ok", "ln_ok"))
        vch = sem("v_chain0")

        @block.sync
        def _(sp):
            m["start"](sp)
            for s in range(2):
                src = a["x"].rearrange("(r s) t -> s r t", s=2)[s]
                sp.dma_start(tok[s * C:(s + 1) * C], src.partition_broadcast(C)).then_inc(ld_x, 16)
            for n, w in enumerate(("L0_tok_Wq", "L0_tok_Wk", "L0_tok_Wv", "L0_tok_Wo")):
                sp.dma_start(w_nat[:, n], a[w].rearrange("(k p) i -> p k i", p=P)).then_inc(ld_w, 16)

        @block.scalar
        def _(act):
            act.dma_start(emb_w[:], a["L0_tok_emb_W"].rearrange("(k p) c -> p k c", p=P)).then_inc(ld_e, 16)
            act.dma_start(emb_bc[:], a["L0_tok_emb_b"].rearrange("(k p) -> p k", p=P), allow_slow_non_contiguous=True).then_inc(ld_e, 16)
            act.dma_start(bqk[:, 0], a["L0_tok_bq"].rearrange("(k p) -> p k", p=P), allow_slow_non_contiguous=True).then_inc(ld_e, 16)
            act.dma_start(bqk[:, 1], a["L0_tok_bk"].rearrange("(k p) -> p k", p=P), allow_slow_non_contiguous=True).then_inc(ld_e, 16)
            act.dma_start(bv_b[:], bcast_rows(a["L0_tok_bv"])).then_inc(ld_e, 16)
            act.dma_start(bo_b[:], bcast_rows(a["L0_tok_bo"])).then_inc(ld_e, 16)
            for n in range(4):
                act.wait_ge(w_tp, START + n + 1)
                nc.scalar.copy(w_t[:, n], ps[n][:].rearrange("p (k o) -> p k o", k=KT)).then_inc(w_cp, 1)
            act.wait_ge(c1_ok, START + 1)
            nc.scalar.activation(cnt1[:], cnt1[:], ACT.Ln).then_inc(ln_ok, 1)
            for k in range(KT):
                act.wait_ge(s_mm, START + k + 1)
                nc.scalar.copy(score[:, k * GB:(k + 1) * GB], ps[2 + k][:].rearrange("p (h c) -> p h c", c=C))
            for k in range(2):
                act.wait_ge(c_mm, START + k + 1)
                nc.scalar.copy(logc[:, k * PAIRS // 2:(k + 1) * PAIRS // 2], ps[6 + k][:].rearrange("p (r c) -> p r c", c=C))

        @block.gpsimd
        def _(pool):
            pch = Chain(pool, sem("p_chain0"))
            pch.link(nc.gpsimd.memset(ident[:], 0.0))
            pch.link(nc.gpsimd.affine_select(out=ident[:], in_=ident[:], compare_op=ALU.not_equal, fill=1.0,
                                             base=0, pattern=[[-1, P]], channel_multiplier=1))
            for s in range(2):
                pch.link(nc.gpsimd.iota(cid[s * C:(s + 1) * C], pattern=[[0, 1]], base=0, channel_multiplier=1,
                                        allow_small_or_imprecise_dtypes=True))
            pch.link(nc.gpsimd.memset(m["mhalf"][:], -0.5))
            for s in range(2):
                pch.link(nc.gpsimd.memset(row_half[s * C:(s + 1) * C, s:s + 1], 1.0))
                pch.link(nc.gpsimd.memset(row_half[s * C:(s + 1) * C, 1 - s:2 - s], 0.0))
            pch.link(nc.gpsimd.memset(col_head[:], 1.0))
            pch.link(nc.gpsimd.affine_select(out=col_head[:], in_=col_head[:], compare_op=ALU.is_ge, fill=0.0,
                                             base=0, pattern=[[-D, GB]], channel_multiplier=1))
            pch.link(nc.gpsimd.affine_select(out=col_head[:], in_=col_head[:], compare_op=ALU.is_ge, fill=0.0,
                                             base=D - 1, pattern=[[D, GB]], channel_multiplier=-1))
            pch.link(nc.gpsimd.memset(same_half[:], 0.0))
            for s in range(2):
                pch.link(nc.gpsimd.memset(same_half[s * C:(s + 1) * C, s * C:(s + 1) * C], 1.0))
            nc.gpsimd.tensor_tensor(ident64[:], ident[:, 0:C], ident[:, C:P], ALU.add).then_inc(masks, 1)

        @block.vector
        def _(dve):
            ch = Chain(dve, vch)
            dve.wait_ge(ld_e, START + 96)
            for k in range(KT):
                for s in range(2):
                    last = nc.vector.tensor_scalar(emb_t[:, k, s * C:(s + 1) * C], emb_w[:, k], emb_bc[:, k:k + 1],
                                                   None, ALU.add)
            last.then_inc(emb_ok, 1)
            dve.wait_ge(masks, START + 1)
            dve.wait_ge(ld_x, START + 32)
            ch.link(nc.vector.tensor_scalar(onehot[:], tok[:], cid[:, 0:1], None, ALU.is_equal))
            ch.link(nc.vector.reduce_sum(cnt[:], onehot[:], AX.X))
            nc.vector.tensor_scalar(cnt1[:], cnt[:], 1.0, None, ALU.max).then_inc(c1_ok, 1)
            nc.vector.tensor_scalar(absent[:], cnt[:], 1.0, 0.0, ALU.subtract, ALU.min)
            dve.wait_ge(q_mm, START + 1)
            for k in range(KT):
                last = nc.vector.tensor_scalar(q_t[:, k], ps[4][:, k * P:(k + 1) * P], bqk[:, 0, k:k + 1],
                                               float(D) ** -0.5, ALU.add, ALU.mult)
            last.then_inc(q_ok, 1)
            for k in range(KT):
                ch.link(nc.vector.tensor_scalar(k_t[:, k], ps[4][:, 2 * P + k * C:2 * P + (k + 1) * C],
                                                bqk[:, 1, k:k + 1], None, ALU.add))
            for k in range(KT):
                last = nc.vector.tensor_tensor(k_heads[:, k], k_t[:, k].unsqueeze(1).broadcast_to([P, GB, C]),
                                               col_head[:].unsqueeze(2).broadcast_to([P, GB, C]), ALU.mult)
            last.then_inc(k_ok, 1)
            dve.wait_ge(ln_ok, START + 1)
            ch.link(nc.vector.scalar_tensor_tensor(cnt1[:], absent[:], BIG, cnt1[:], ALU.mult, ALU.add))
            nc.vector.tensor_tensor(log_diag[:], ident64[:].unsqueeze(1).broadcast_to([P, PAIRS, C]),
                                    cnt1[:].unsqueeze(2).broadcast_to([P, PAIRS, C]), ALU.mult).then_inc(c_dg, 1)
            dve.wait_ge(e_tp, START + 1)
            ch.link(nc.vector.tensor_tensor(v_tab[:], ps[5][:, 0:E], bv_b[:], ALU.add))
            half = row_half[:].unsqueeze(1)
            nc.vector.tensor_tensor(v_pair[:, :, 0:2 * D].rearrange("p g (s d) -> p g s d", d=D),
                                    v_tab[:].rearrange("p (g s d) -> p g s d", s=2, d=D),
                                    half.unsqueeze(3).broadcast_to([P, HP, 2, D]), ALU.mult)
            ch.link(nc.vector.tensor_copy(v_pair[:, :, 2 * D:], half.broadcast_to([P, HP, 2])))
            ch.link(nc.vector.tensor_tensor(base[:], ps[5][:, E:2 * E], bo_b[:], ALU.add))

        @block.tensor
        def _(pe):
            pe.wait_ge(masks, START + 1)
            for n in range(4):
                pe.wait_ge(ld_w, START + 16 * 4)
                for ki in range(KT):
                    for ko in range(KT):
                        last = nc.tensor.transpose(ps[n][:, ki * E + ko * P:ki * E + (ko + 1) * P],
                                                   w_nat[:, n, ko, ki * P:(ki + 1) * P], ident[:])
                last.then_inc(w_tp, 1)
            pe.wait_ge(emb_ok, START + 1)
            pe.wait_ge(w_cp, START + 4)
            for ko in range(KT):
                for ki in range(KT):
                    nc.tensor.matmul(ps[4][:, ko * P:(ko + 1) * P], w_t[:, 0, ki, ko * P:(ko + 1) * P], emb_t[:, ki],
                                     start=ki == 0, stop=ki == KT - 1)
            for ko in range(KT):
                for ki in range(KT):
                    last = nc.tensor.matmul(ps[4][:, 2 * P + ko * C:2 * P + (ko + 1) * C],
                                            w_t[:, 1, ki, ko * P:(ko + 1) * P], emb_t[:, ki, 0:C],
                                            start=ki == 0, stop=ki == KT - 1)
            last.then_inc(q_mm, 1)
            for ki in range(KT):
                nc.tensor.matmul(ps[5][:, 0:E], emb_t[:, ki], w_t[:, 2, ki], start=ki == 0, stop=ki == KT - 1)
            for k in range(KT):
                last = nc.tensor.transpose(ps[5][:, E + k * P:E + (k + 1) * P], emb_t[:, k], ident[:])
            last.then_inc(e_tp, 1)
            pe.wait_ge(q_ok, START + 1)
            pe.wait_ge(k_ok, START + 1)
            for k in range(KT):
                nc.tensor.matmul(ps[2 + k][:], q_t[:, k], k_heads[:, k].rearrange("p h c -> p (h c)"),
                                 start=True, stop=True).then_inc(s_mm, 1)
            pe.wait_ge(c_dg, START + 1)
            for k in range(2):
                nc.tensor.matmul(ps[6 + k][:], same_half[:],
                                 log_diag[:, k * PAIRS // 2:(k + 1) * PAIRS // 2].rearrange("p r c -> p (r c)"),
                                 start=True, stop=True).then_inc(c_mm, 1)

    with ExitStack() as ctx:
        def sbx(n, s):
            return ctx.enter_context(nc.sbuf_tensor(n, s, F32))
        logit = [sbx(f"logit{i}", [P, H, C]) for i in range(2)]
        prob = [sbx(f"prob{i}", [P, H * C]) for i in range(2)]
        prob_t = [sbx(f"prob_t{i}", [P, HP, P]) for i in range(2)]
        top = [sbx(f"top{i}", [P, H]) for i in range(2)]
        rden = [sbx(f"rden{i}", [P, HP, 2]) for i in range(2)]
        cx = [sbx(f"cx{i}", [P, E]) for i in range(2)]
        cx_t = [sbx(f"cx_t{i}", [P, KT, P]) for i in range(2)]
        bn = [sbx(f"bn{i}", [P, 6]) for i in range(2)]
        yrow = [sbx(f"yrow{i}", [P, E]) for i in range(2)]
        ps_t = [ctx.enter_context(nc.psum_tensor(f"ps_t{i}", [P, HP * P], F32)) for i in range(2)]
        ps_c = [ctx.enter_context(nc.psum_tensor(f"ps_c{i}", [P, 512], F32)) for i in range(2)]
        ps_y = [ctx.enter_context(nc.psum_tensor(f"ps_y{i}", [P, 512], F32)) for i in range(2)]
        block = ctx.enter_context(nc.Block())

        def par(name):
            return [sem(f"{name}{i}") for i in range(2)]
        lg_ok, ex_ok, pt_mm, pt_ok, cx_mm, cx_ok, ct_mm, ct_ok, y_mm, y_ok = (
            par(n) for n in ("lg_ok", "ex_ok", "pt_mm", "pt_ok", "cx_mm", "cx_ok", "ct_mm", "ct_ok", "y_mm", "y_ok"))
        sc_ok = par("sc_ok")
        TURNS = PAIRS // 2

        @block.sync
        def _(sp):
            m["start"](sp)

        @block.gpsimd
        def _(pool):
            with nc.gpsimd.Fori(0, TURNS) as i:
                for s in range(2):
                    pool.wait_ge(ex_ok[s], START + i)
                    nc.gpsimd.tensor_tensor(logit[s][:], score[:],
                                            logc[:, bass.ds(2 * i + s, 1)].broadcast_to([P, H, C]), ALU.add)\
                        .then_inc(sc_ok[s], 1)

        @block.vector
        def _(dve):
            ch = Chain(dve, sem("v_chain1"))

            def softmax_input(i, s):
                dve.wait_ge(sc_ok[s], START + i + 1)
                ch.link(nc.vector.reduce_max(top[s][:], logit[s][:], AX.X))
                nc.vector.tensor_tensor(logit[s][:], logit[s][:], top[s][:].unsqueeze(2).broadcast_to([P, H, C]),
                                        ALU.subtract).then_inc(lg_ok[s], 1)

            def finish(i, s):
                dve.wait_ge(cx_mm[s], START + i + 1)
                c = ps_c[s][:, 0:HP * (2 * D + 2)].rearrange("p (g n) -> p g n", g=HP)
                ch.link(nc.vector.reciprocal(rden[s][:], c[:, :, 2 * D:]))
                nc.vector.tensor_tensor(cx[s][:].rearrange("p (g s d) -> p g s d", s=2, d=D),
                                        c[:, :, 0:2 * D].rearrange("p g (s d) -> p g s d", d=D),
                                        rden[s][:].unsqueeze(3).broadcast_to([P, HP, 2, D]),
                                        ALU.mult).then_inc(cx_ok[s], 1)

            def output(i, s, r):
                dve.wait_ge(y_mm[s], START + i + 1)
                ch.link(nc.vector.tensor_tensor(yrow[s][:], ps_y[s][:, E:2 * E], base[:], ALU.add))
                ch.link(nc.vector.bn_stats(bn[s][:], yrow[s][:]))
                nc.vector.tensor_copy(stats6[:, bass.ds(r, 1)], bn[s][:].unsqueeze(1))
                nc.vector.tensor_copy(h_tab[:, bass.ds(r, 1)], yrow[s][:].unsqueeze(1)).then_inc(y_ok[s], 1)

            def step(t, new=True, older=True):
                if new:
                    softmax_input(t, 0)
                if older:
                    for s in range(2):
                        finish(t - 2, s)
                if new:
                    softmax_input(t, 1)
                if older:
                    for s in range(2):
                        output(t - 2, s, 2 * (t - 2) + s)

            step(0, older=False)
            step(1, older=False)
            with nc.vector.Fori(2, TURNS) as t:
                ch.enter(t, 2 * 4, 2)
                step(t)
            ch.leave(TURNS)
            step(TURNS, new=False)
            step(TURNS + 1, new=False)

        @block.scalar
        def _(act):
            def exponential(i, s):
                act.wait_ge(lg_ok[s], START + i + 1)
                act.wait_ge(pt_mm[s], START + i)
                nc.scalar.activation(prob[s][:], logit[s][:].rearrange("p h c -> p (h c)"),
                                     ACT.Exp).then_inc(ex_ok[s], 1)

            def copy_prob(i, s):
                act.wait_ge(pt_mm[s], START + i + 1)
                act.wait_ge(cx_mm[s], START + i)
                nc.scalar.copy(prob_t[s][:].rearrange("p g c -> p (g c)"), ps_t[s][:]).then_inc(pt_ok[s], 1)

            def copy_context(i, s):
                act.wait_ge(ct_mm[s], START + i + 1)
                act.wait_ge(y_mm[s], START + i)
                nc.scalar.copy(cx_t[s][:].rearrange("p k c -> p (k c)"), ps_y[s][:, 0:E]).then_inc(ct_ok[s], 1)

            def step(t, new=True, old=True, older=True):
                if old:
                    copy_prob(t - 1, 0)
                if new:
                    exponential(t, 0)
                if old:
                    copy_prob(t - 1, 1)
                if older:
                    for s in range(2):
                        copy_context(t - 2, s)
                if new:
                    exponential(t, 1)

            step(0, old=False, older=False)
            step(1, older=False)
            with nc.scalar.Fori(2, TURNS) as t:
                step(t)
            step(TURNS, new=False)
            step(TURNS + 1, new=False, old=False)

        @block.tensor
        def _(pe):
            def transpose_prob(i, s):
                pe.wait_ge(ex_ok[s], START + i + 1)
                pe.wait_ge(pt_ok[s], START + i)
                for g in range(HP):
                    last = nc.tensor.transpose(ps_t[s][:, g * P:(g + 1) * P], prob[s][:, g * P:(g + 1) * P], ident[:])
                last.then_inc(pt_mm[s], 1)

            def context(i, s):
                pe.wait_ge(pt_ok[s], START + i + 1)
                pe.wait_ge(cx_ok[s], START + i)
                n = 2 * D + 2
                for g in range(HP):
                    last = nc.tensor.matmul(ps_c[s][:, g * n:(g + 1) * n], prob_t[s][:, g], v_pair[:, g],
                                            start=True, stop=True)
                last.then_inc(cx_mm[s], 1)

            def transpose_context(i, s):
                pe.wait_ge(cx_ok[s], START + i + 1)
                pe.wait_ge(y_ok[s], START + i)
                for k in range(KT):
                    last = nc.tensor.transpose(ps_y[s][:, k * P:(k + 1) * P], cx[s][:, k * P:(k + 1) * P], ident[:])
                last.then_inc(ct_mm[s], 1)

            def project(i, s):
                pe.wait_ge(ct_ok[s], START + i + 1)
                for k in range(KT):
                    last = nc.tensor.matmul(ps_y[s][:, E:2 * E], cx_t[s][:, k], w_t[:, 3, k],
                                            start=k == 0, stop=k == KT - 1)
                last.then_inc(y_mm[s], 1)

            def step(t, new=True, old=True):
                for s in range(2):
                    if old:
                        context(t - 1, s)
                    if new:
                        transpose_prob(t, s)
                if old:
                    for s in range(2):
                        transpose_context(t - 1, s)
                    for s in range(2):
                        project(t - 1, s)

            step(0, old=False)
            with nc.tensor.Fori(1, TURNS) as t:
                step(t)
            step(TURNS, new=False)


CHUNKS = [(0, False)] + [c for d in range(1, D // 2) for c in ((d, False), (d, True))] + [(D // 2, False)]
N = len(CHUNKS)
NF = D // 2 + 1


def shift(c):
    d, mirrored = CHUNKS[c]
    return D - d if mirrored else d


def pieces(s):
    return [(0, D - s, s)] + ([(D - s, D, s - D)] if s else [])


def part(m, g, j, lo, hi):
    return m["inp"][:, bass.ds(g % 2, 1), j, lo * T:hi * T].rearrange("p o n -> p (o n)")


def multiply_updates(nc, m, g, c):
    for lo, hi, off in pieces(shift(c)):
        last = nc.gpsimd.tensor_tensor(m["upd"][c % 2][:, lo * T:hi * T], part(m, g, 3, lo, hi),
                                       part(m, g, 1, lo + off, hi + off), ALU.mult)
    last.then_inc(m["upd_ok"], 1)


def multiply_factors(nc, m, g, f):
    rows = D if f < D // 2 else D // 2
    for lo, hi, off in pieces(f):
        if lo < rows:
            last = nc.vector.tensor_tensor(m["prod"][:, lo * T:hi * T], part(m, g, 2, lo, hi),
                                           part(m, g, 1, lo + off, hi + off), ALU.mult)
    last.then_inc(m["prod_ok"], 1)


def recurrent_inputs(nc, a, m, sem, sb):
    ident, onehot, h_tab, g_tab = m["ident"], m["onehot"], m["h_tab"], m["g_tab"]
    cnt, stats6, same_half, rec_in = m["cnt"], m["stats6"], m["same_half"], m["rec_in"]
    w_all = sb("w_all", [P, KT, NPROJ])
    wn = sb("wn", [P, PAIRS])
    wm = sb("wm", [P, 2, PAIRS])
    dm = sb("dm", [P, PAIRS])
    mean_row, var_row = sb("mean_row", [P, PAIRS]), sb("var_row", [P, PAIRS])
    ex2 = sb("ex2", [P, PAIRS])
    mean_b = sb("mean_b", [P, PAIRS])
    varb = sb("varb", [P, PAIRS])
    rstd_b = sb("rstd_b", [P, PAIRS])
    mean_1 = sb("mean_1", [P, PAIRS])
    var1 = sb("var1", [P, PAIRS])
    rstd_1 = sb("rstd_1", [P, PAIRS])

    with ExitStack() as ctx:
        ps = ctx.enter_context(nc.psum_tensor("st_ps", [P, 2, 512], F32))
        block = ctx.enter_context(nc.Block())
        ld_a, w_ok, sum_mm = (sem(n) for n in ("ld_a", "w_ok", "sum_mm"))

        @block.sync
        def _(sp):
            m["start"](sp)
            for n, w in enumerate(("L0_attn_Wq", "L0_attn_Wk", "L0_attn_Wv", "L0_attn_Wg")):
                sp.dma_start(w_all[:, :, n * E:(n + 1) * E], a[w].rearrange("(k p) o -> p k o", p=P)).then_inc(ld_a, 16)
            sp.dma_start(w_all[:, :, 4 * E:], a["L0_attn_Wbeta"].rearrange("(k p) o -> p k o", p=P)).then_inc(ld_a, 16)
            sp.wait_ge(ld_a, START + 16 * 5)

        @block.vector
        def _(dve):
            ch = Chain(dve, sem("v_chain2"))
            mean_r, var_r = mean_row[:], var_row[:]
            ch.link(row_statistics(nc, ch, stats6[:], mean_r, var_r, dm[:], 0.0))
            ch.link(nc.vector.tensor_scalar(wn[:], cnt[:], 1.0 / T, None, ALU.mult))
            nc.vector.tensor_tensor(wm[:, 0], wn[:], mean_r, ALU.mult).then_inc(w_ok, 1)
            dve.wait_ge(sum_mm, START + 1)
            ch.link(nc.vector.tensor_copy(mean_b[:], ps[:, 0, 0:PAIRS]))
            ch.link(nc.vector.tensor_tensor(dm[:], mean_r, mean_b[:], ALU.subtract))
            ch.link(nc.vector.tensor_tensor(ex2[:], dm[:], dm[:], ALU.mult))
            ch.link(nc.vector.tensor_tensor(ex2[:], ex2[:], var_r, ALU.add))
            nc.vector.tensor_tensor(wm[:, 1], wn[:], ex2[:], ALU.mult).then_inc(w_ok, 1)
            dve.wait_ge(sum_mm, START + 2)
            ch.link(nc.vector.tensor_scalar(varb[:], ps[:, 1, 0:PAIRS], EPS, None, ALU.add))
            inverse_root(nc, ch, varb[:], rstd_b[:], ex2[:])
            ch.link(nc.vector.tensor_tensor(mean_1[:], dm[:], rstd_b[:], ALU.mult))
            ch.link(nc.vector.tensor_tensor(var1[:], var_r, rstd_b[:], ALU.mult))
            ch.link(nc.vector.tensor_tensor(var1[:], var1[:], rstd_b[:], ALU.mult))
            ch.link(nc.vector.tensor_scalar(var1[:], var1[:], EPS, None, ALU.add))
            inverse_root(nc, ch, var1[:], rstd_1[:], ex2[:])

        @block.tensor
        def _(pe):
            for n in range(2):
                pe.wait_ge(w_ok, START + n + 1)
                nc.tensor.matmul(ps[:, n, 0:PAIRS], same_half[:], wm[:, n], start=True, stop=True).then_inc(sum_mm, 1)

    with ExitStack() as ctx:
        def sbx(n, s):
            return ctx.enter_context(nc.sbuf_tensor(n, s, F32))
        x1 = [sbx(f"x1_{i}", [P, E]) for i in range(2)]
        x1_t = [sbx(f"x1_t{i}", [P, KT, P]) for i in range(2)]
        raw = [sbx(f"raw{i}", [P, 2 * E]) for i in range(2)]
        sq = [sbx(f"sq{i}", [P, 2 * H, D]) for i in range(2)]
        norm2 = [sbx(f"norm2_{i}", [P, 2 * H]) for i in range(2)]
        newton = [sbx(f"newton{i}", [P, 2 * H]) for i in range(2)]
        rnorm = [sbx(f"rnorm{i}", [P, 2 * H]) for i in range(2)]
        beta = [sbx(f"beta{i}", [P, H]) for i in range(2)]
        sig = [sbx(f"sig{i}", [P, E]) for i in range(2)]
        tab = [sbx(f"tab{i}", [P, 4, E]) for i in range(2)]
        hot = [sbx(f"hot{i}", [P, T]) for i in range(2)]
        feat = m["feat"]
        ps_x = [ctx.enter_context(nc.psum_tensor(f"ps_x{i}", [P, 512], F32)) for i in range(2)]
        ps_qk = ctx.enter_context(nc.psum_tensor("ps_qk", [P, 2 * E], F32))
        ps_vg = ctx.enter_context(nc.psum_tensor("ps_vg", [P, 2 * E], F32))
        ps_f = ctx.enter_context(nc.psum_tensor("ps_f", [P, 2, 4, KT, T], F32))
        block = ctx.enter_context(nc.Block())

        def par(name):
            return [sem(f"{name}{i}") for i in range(2)]
        x_ok, xt_mm, xt_ok, pj_mm, sq_ok, sg_ok, tb_ok, hot_ok, f_mm, f_ok, f_st = (
            par(n) for n in ("x_ok", "xt_mm", "xt_ok", "pj_mm", "sq_ok", "sg_ok", "tb_ok", "hot_ok",
                             "f_mm", "f_ok", "f_st"))
        vg_free, ld_g = par("vg_free"), sem("ld_g")
        m["f_st"], m["ld_g"], m["upd_ok"], m["prod_ok"] = f_st, ld_g, sem("upd_ok"), sem("prod_ok")
        TURNS = PAIRS // 2

        @block.vector
        def _(dve):
            ch = Chain(dve, sem("v_chain3"))

            def rows(i, s, r):
                h = h_tab[:, bass.ds(r, 1)]
                ch.link(nc.vector.tensor_scalar(h, h, mean_b[:, bass.ds(r, 1)], rstd_b[:, bass.ds(r, 1)],
                                                ALU.subtract, ALU.mult))
                dve.wait_ge(xt_mm[s], START + i)
                nc.vector.tensor_scalar(x1[s][:].unsqueeze(1), h, mean_1[:, bass.ds(r, 1)], rstd_1[:, bass.ds(r, 1)],
                                        ALU.subtract, ALU.mult).then_inc(x_ok[s], 1)

            def values(i, s, r):
                dve.wait_ge(sg_ok[s], START + i + 1)
                dve.wait_ge(f_mm[s], START + i)
                nc.vector.tensor_tensor(tab[s][:, 3].rearrange("p (h d) -> p h d", d=D),
                                        ps_vg[:, 0:E].rearrange("p (h d) -> p h d", d=D),
                                        beta[s][:].unsqueeze(2).broadcast_to([P, H, D]), ALU.mult)
                nc.vector.tensor_tensor(g_tab[:, bass.ds(r, 1)], ps_vg[:, E:].unsqueeze(1), sig[s][:].unsqueeze(1), ALU.mult)\
                    .then_inc(vg_free[s], 1)

            def norms(i, s):
                dve.wait_ge(sq_ok[s], START + i + 1)
                ch.link(nc.vector.reduce_sum(norm2[s][:], sq[s][:], AX.X))
                ch.link(nc.vector.tensor_scalar(norm2[s][:], norm2[s][:], 1e-24, None, ALU.max))
                inverse_root(nc, ch, norm2[s][:], rnorm[s][:], newton[s][:])

            def table(s):
                ch.link(nc.vector.tensor_tensor(tab[s][:, 0:2].rearrange("p j (h d) -> p (j h) d", d=D),
                                                raw[s][:].rearrange("p (h d) -> p h d", d=D),
                                                rnorm[s][:].unsqueeze(2).broadcast_to([P, 2 * H, D]), ALU.mult))
                nc.vector.tensor_tensor(tab[s][:, 2].rearrange("p (h d) -> p h d", d=D),
                                        tab[s][:, 1].rearrange("p (h d) -> p h d", d=D),
                                        beta[s][:].unsqueeze(2).broadcast_to([P, H, D]), ALU.mult).then_inc(tb_ok[s], 1)

            def step(t, new=True, old=True):
                for s in range(2):
                    if new:
                        rows(t, s, 2 * t + s)
                for s in range(2):
                    if old:
                        values(t - 1, s, 2 * (t - 1) + s)
                        norms(t - 1, s)
                        table(s)

            step(0, old=False)
            with nc.vector.Fori(1, TURNS) as t:
                ch.enter(t, 2 * (1 + 13 + 1), 1)
                step(t)
            ch.leave(TURNS)
            step(TURNS, new=False)
            dve.wait_ge(ld_g, START + 64)
            multiply_factors(nc, m, 0, 0)

        @block.gpsimd
        def _(pool):
            with nc.gpsimd.Fori(0, TURNS) as i:
                for s in range(2):
                    pool.wait_ge(f_mm[s], START + i)
                    nc.gpsimd.tensor_copy(hot[s][:].unsqueeze(1), onehot[:, bass.ds(2 * i + s, 1)]).then_inc(hot_ok[s], 1)
            pool.wait_ge(ld_g, START + 64)
            for c in range(2):
                multiply_updates(nc, m, 0, c)

        @block.scalar
        def _(act):
            def copy_rows(i, s):
                act.wait_ge(xt_mm[s], START + i + 1)
                act.wait_ge(pj_mm[s], START + i)
                nc.scalar.copy(x1_t[s][:].rearrange("p k c -> p (k c)"), ps_x[s][:, 0:E]).then_inc(xt_ok[s], 1)

            def squares(i, s):
                act.wait_ge(pj_mm[s], START + i + 1)
                act.wait_ge(tb_ok[s], START + i)
                nc.scalar.activation(beta[s][:], ps_x[s][:, E:E + H], ACT.Sigmoid)
                nc.scalar.activation(sig[s][:], ps_vg[:, E:], ACT.Sigmoid).then_inc(sg_ok[s], 1)
                nc.scalar.copy(raw[s][:], ps_qk[:])
                nc.scalar.square(sq[s][:], ps_qk[:].rearrange("p (h d) -> p h d", d=D)).then_inc(sq_ok[s], 1)

            def copy_features(i, s):
                act.wait_ge(f_mm[s], START + i + 1)
                act.wait_ge(f_st[s], START + 32 * i)
                for q in range(2):
                    ins = nc.scalar.copy(feat[s][:, q], ps_f[:, q])
                ins.then_inc(f_ok[s], 1)

            def step(t, new=True, old=True, older=True):
                if old:
                    squares(t - 1, 0)
                if older:
                    copy_features(t - 2, 1)
                if new:
                    copy_rows(t, 0)
                if old:
                    squares(t - 1, 1)
                    copy_features(t - 1, 0)
                if new:
                    copy_rows(t, 1)

            step(0, old=False, older=False)
            step(1, older=False)
            with nc.scalar.Fori(2, TURNS) as t:
                step(t)
            step(TURNS, new=False)
            step(TURNS + 1, new=False, old=False)

        @block.tensor
        def _(pe):
            def transpose_rows(i, s):
                pe.wait_ge(x_ok[s], START + i + 1)
                pe.wait_ge(sg_ok[s], START + i)
                for k in range(KT):
                    last = nc.tensor.transpose(ps_x[s][:, k * P:(k + 1) * P], x1[s][:, k * P:(k + 1) * P], ident[:])
                last.then_inc(xt_mm[s], 1)

            def project(i, s):
                pe.wait_ge(xt_ok[s], START + i + 1)
                pe.wait_ge(sq_ok[1 - s], START + i + s)
                pe.wait_ge(vg_free[1 - s], START + i + s)
                for dst, lo, n in ((ps_qk[:], 0, 2 * E), (ps_vg[:], 2 * E, 2 * E), (ps_x[s][:, E:E + H], 4 * E, H)):
                    for k in range(KT):
                        last = nc.tensor.matmul(dst, x1_t[s][:, k], w_all[:, k, lo:lo + n],
                                                start=k == 0, stop=k == KT - 1)
                last.then_inc(pj_mm[s], 1)

            def to_positions(i, s):
                pe.wait_ge(tb_ok[s], START + i + 1)
                pe.wait_ge(hot_ok[s], START + i + 1)
                pe.wait_ge(f_ok[1 - s], START + i + s)
                for j in range(4):
                    for k in range(KT):
                        for q in range(2):
                            rows = slice(q * C, (q + 1) * C)
                            last = nc.tensor.matmul(ps_f[:, q, j, k], tab[s][rows, j, k * P:(k + 1) * P],
                                                    hot[s][rows], start=True, stop=True)
                last.then_inc(f_mm[s], 1)

            def step(t, new=True, old=True, older=True):
                if old:
                    project(t - 1, 0)
                if older:
                    to_positions(t - 2, 1)
                if new:
                    transpose_rows(t, 0)
                if old:
                    project(t - 1, 1)
                    to_positions(t - 1, 0)
                if new:
                    transpose_rows(t, 1)

            step(0, old=False, older=False)
            step(1, older=False)
            with nc.tensor.Fori(2, TURNS) as t:
                step(t)
            step(TURNS, new=False)
            step(TURNS + 1, new=False, old=False)

        @block.sync
        def _(sp):
            m["start"](sp)
            dst = rec_in.rearrange("b j (k p) t -> b p (j k) t", p=P)

            def store(i):
                for s in range(2):
                    sp.wait_ge(f_ok[s], START + i + 1)
                    for q in range(2):
                        sp.dma_start(dst[bass.ds(4 * i + 2 * s + q, 1)].rearrange("b p n t -> (b p) n t"),
                                     feat[s][:, q].rearrange("p j k t -> p (j k) t")).then_inc(f_st[s], 16)

            own = GB // 4
            with nc.sync.Fori(0, own) as i:
                store(i)
            with nc.sync.Fori(own, own + 4) as i:
                store(i)
                for s in range(2):
                    sp.wait_ge(f_st[s], START + 32 * own)
                load_group(sp, m, 0, 0, i - own, ld_g)
            with nc.sync.Fori(own + 4, TURNS) as i:
                store(i)


def load_group(eng, m, g, par, j, done):
    src = m["rec_in"].rearrange("(g b) j (h i) t -> g j b h (i t)", b=GB, h=H)
    eng.dma_start(m["inp"][:, bass.ds(par, 1), bass.ds(j, 1)].rearrange("p o u n -> p (o u n)"),
                  src[bass.ds(g, 1), bass.ds(j, 1)].rearrange("g j b h n -> (g j b) h n")).then_inc(done, 16)


def recurrence(nc, a, m, sem, sb, pb):
    ident, rec_out = m["ident"], m["rec_out"]
    osb, ld_g, f_st = m["osb"], m["ld_g"], m["f_st"]
    upd, prod, upd_ok, prod_ok = m["upd"], m["prod"], m["upd_ok"], m["prod_ok"]
    state = [sb(f"state{i}", [P, RT]) for i in range(3)]
    read = [sb(f"read{i}", [P, RT]) for i in range(2)]
    ps_a = pb("ps_a", RT)
    ps_o = pb("ps_o", RT)

    with ExitStack() as ctx:
        block = ctx.enter_context(nc.Block())
        upd_free, fac_ok, read_ok, read_free, o_ok, o_st = (
            sem(n) for n in ("upd_free", "fac_ok", "read_ok", "read_free", "rec_ok", "rec_st"))
        a_zero, o_w, o_ld = sem("a_zero"), sem("o_w"), sem("o_ld")
        m["o_st"], m["o_w"], m["o_ld"] = o_st, o_w, o_ld

        @block.sync
        def _(sp):
            m["start"](sp)
            for s in range(2):
                sp.wait_ge(f_st[s], START + 32 * (PAIRS // 2))
            with nc.sync.Fori(1, GROUPS) as g:
                sp.wait_ge(ld_g, START + 64 * g)
                sp.wait_ge(read_ok, START + (g - 1) * N)
                sp.wait_ge(upd_ok, START + (g - 1) * N)
                for j in range(4):
                    load_group(sp, m, g, g % 2, j, ld_g)
                sp.wait_ge(o_ok, START + g)
                sp.dma_start(rec_out.rearrange("(g b) (h i) t -> g (b h) (i t)", b=GB, h=H)[bass.ds(g - 1, 1)]
                             .rearrange("g p n -> (g p) n"), osb[:]).then_inc(o_st, 16)
            load_output_constants(sp, a, m, o_w)
            load_quad(sp, m, 0)
            sp.wait_ge(o_ok, START + GROUPS)
            sp.dma_start(rec_out.rearrange("(g b) (h i) t -> g (b h) (i t)", b=GB, h=H)[GROUPS - 1], osb[:])\
                .then_inc(o_st, 16)

        @block.gpsimd
        def _(pool):
            def updates(g, c):
                pool.wait_ge(upd_free, START + g * N + c + 1)
                multiply_updates(nc, m, g, c)

            for c in range(2, N):
                updates(0, c)
            with nc.gpsimd.Fori(1, GROUPS) as g:
                pool.wait_ge(ld_g, START + g * 64 + 64)
                for c in range(N):
                    updates(g, c)

        @block.scalar
        def _(act):
            def copy_out(g):
                act.wait_ge(read_free, START + g * N + N + 2)
                act.wait_ge(o_st, START + g * 16)
                nc.scalar.copy(osb[:], ps_o[:]).then_inc(o_ok, 1)

            act.wait_ge(a_zero, START + 1)
            def factors(g, which):
                for f in which:
                    act.wait_ge(prod_ok, START + g * NF + f + 1)
                    act.wait_ge(upd_free, START + g * N + sum(d < f for d, _ in CHUNKS) + 2)
                    rows = D if f < D // 2 else D // 2
                    nc.scalar.activation(ps_a[:, 0:rows * T].rearrange("p (i t) -> p i t", t=T)[:, :, 1:],
                                         prod[:, 0:rows * T].rearrange("p (i t) -> p i t", t=T)[:, :, 1:],
                                         ACT.Copy, bias=1.0, scale=-1.0).then_inc(fac_ok, 1)

            factors(0, range(NF))
            with nc.scalar.Fori(1, GROUPS) as g:
                factors(g, [0])
                copy_out(g - 1)
                factors(g, range(1, NF))
            copy_out(GROUPS - 1)

        @block.vector
        def _(dve):
            ch = Chain(dve, sem("v_chain4"))
            ch.link(nc.vector.memset(ps_a[:].rearrange("p (i t) -> p i t", t=T)[:, :, 0], 0.0))
            dve.sem_inc(upd_free, 2)
            dve.sem_inc(a_zero, 1)

            def products(g, f):
                dve.wait_ge(fac_ok, START + g * NF + f)
                multiply_factors(nc, m, g, f)

            def state_of(c):
                return state[1 if c == N - 1 else c % 3]

            def scan(g, c):
                d, mirrored = CHUNKS[c]
                if not mirrored:
                    dve.wait_ge(fac_ok, START + g * NF + d + 1)
                dve.wait_ge(upd_ok, START + g * N + c + 1)
                dve.wait_ge(read_ok, START + g * N + (c - 1 if c in (1, N - 1) else c - 2))
                if mirrored:
                    runs = [(d, D, 0), (0, d, D - d)]
                elif d == D // 2:
                    runs = [(0, d, 0), (d, D, 0)]
                else:
                    runs = [(0, D, 0)]
                for lo, hi, f0 in runs:
                    ins = nc.vector.tensor_tensor_scan(state_of(c)[:, lo * T:hi * T],
                                                       ps_a[:, f0 * T:(f0 + hi - lo) * T],
                                                       upd[c % 2][:, lo * T:hi * T], 0.0, ALU.mult, ALU.add)
                ins.then_inc(upd_free, 1)

            def readout(g, c):
                dve.wait_ge(upd_free, START + g * N + c + 3)
                dve.wait_ge(read_free, START + g * N + c + 1)
                for lo, hi, off in pieces(shift(c)):
                    ins = nc.vector.tensor_tensor(read[c % 2][:, lo * T:hi * T], state_of(c)[:, lo * T:hi * T],
                                                  part(m, g, 0, lo + off, hi + off), ALU.mult)
                ins.then_inc(read_ok, 1)

            def group(g, next_group=True):
                for c, (d, mirrored) in enumerate(CHUNKS):
                    if d < D // 2 and CHUNKS[c + 1][0] != d:
                        products(g, d + 1)
                    scan(g, c)
                    if c:
                        readout(g, c - 1)
                if next_group:
                    dve.wait_ge(ld_g, START + g * 64 + 128)
                    products(g + 1, 0)
                readout(g, N - 1)

            with nc.vector.Fori(0, GROUPS - 1) as g:
                group(g)
            group(GROUPS - 1, next_group=False)

        @block.tensor
        def _(pe):
            pe.sem_inc(read_free, 2)
            with nc.tensor.Fori(0, GROUPS) as g:
                pe.wait_ge(o_ok, START + g)
                for c in range(N):
                    pe.wait_ge(read_ok, START + g * N + c + 1)
                    for n in range(4):
                        last = nc.tensor.matmul(ps_o[:, n * 512:(n + 1) * 512], ident[:],
                                                read[c % 2][:, n * 512:(n + 1) * 512],
                                                start=c == 0, stop=c == N - 1)
                    last.then_inc(read_free, 1)


def load_output_constants(eng, a, m, done):
    eng.dma_start(m["w_out"][:], a["L0_attn_Wout"].rearrange("(k p) o -> p k o", p=P)).then_inc(done, 16)
    eng.dma_start(m["lng"][:], bcast_rows(a["L0_attn_ln_g"])).then_inc(done, 16)
    eng.dma_start(m["lnb"][:], bcast_rows(a["L0_attn_ln_b"])).then_inc(done, 16)
    eng.dma_start(m["gw"][:], a["L0_ffn_gate_w"]).then_inc(done, 16)
    for j in range(QB):
        eng.dma_start(m["gb"][j * X:(j + 1) * X], a["L0_ffn_gate_b"].unsqueeze(1)).then_inc(done, 16)


def load_quad(eng, m, i):
    eng.dma_start(m["ao"][:].rearrange("p j k t -> p (j k) t"),
                  m["rec_out"][bass.ds(QB * i, QB)].rearrange("b (k p) t -> p (b k) t", p=P)).then_inc(m["o_ld"], 16)


def recurrent_outputs(nc, a, m, sem, sb, replace_tables):
    ident, onehot, h_tab, g_tab, mhalf = m["ident"], m["onehot"], m["h_tab"], m["g_tab"], m["mhalf"]
    h2, picked, merged = m["h2"], m["picked"], m["merged"]
    w_out, lng, lnb, gw, gb = m["w_out"], m["lng"], m["lnb"], m["gw"], m["gb"]
    gw_t = sb("gw_t", [P, KT, X])
    hot = sb("hot_q", [P, QB, T])
    hq = sb("hq", [P, 2, E])
    ao, gq = m["ao"], m["gq"]
    bn = sb("bn_q", [P, QB, 6])
    mean = sb("mean_q", [P, 2, QB])
    tmp = sb("tmp_q", [P, QB])
    idle = sb("idle", [P, TOPK])
    ve = sb("ve_q", [P, 2, QB])
    rs = sb("rs_q", [P, 2, QB])
    z = sb("z_q", [P, QB, E])
    z_t = sb("z_t", [P, QB, KT, P])
    x2 = sb("x2", [P, QB, E])
    x2_t = sb("x2_t", [P, QB, KT, P])
    lg = sb("lg_q", [P, T])
    nmx = sb("nmx", [P, 1])
    den = sb("den", [P, 1])
    rden = sb("rden_q", [P, 1])
    pr = sb("pr", [P, T])
    top8 = sb("top8", [P, TOPK])
    rep = sb("rep", [P, T])
    pm = sb("pm", [P, T])
    pm_t = sb("pm_t", [P, P])

    with ExitStack() as ctx:
        ps_a = ctx.enter_context(nc.psum_tensor("pq_a", [P, QB, E], F32))
        ps_g = ctx.enter_context(nc.psum_tensor("pq_g", [P, QB, E], F32))
        ps_z = ctx.enter_context(nc.psum_tensor("pq_z", [P, QB, E], F32))
        ps_h = ctx.enter_context(nc.psum_tensor("pq_h", [P, QB, E], F32))
        names = ("o_gwt", "o_gwt_ok", "o_hot", "o_at", "o_gt", "o_zn", "o_z", "o_zt",
                 "o_ztok", "o_h", "o_hc", "o_x", "o_xt", "o_xtok", "o_lg", "o_nm", "o_ex", "o_pm", "o_pt", "o_ptok",
                 "o_mm", "o_mc", "o_pmc", "o_zs")
        (o_gwt, o_gwt_ok, o_hot, o_at, o_gt, o_zn, o_z, o_zt, o_ztok, o_h, o_hc, o_x, o_xt,
         o_xtok, o_lg, o_nm, o_ex, o_pm, o_pt, o_ptok, o_mm, o_mc, o_pmc, o_zs) = (sem(n) for n in names)
        w1_ld, w2_ld = ([[sem(f"{n}{s}{h}") for h in range(2)] for s in range(2)] for n in ("w1_ld", "w2_ld"))
        o_ld, o_w, o_st = m["o_ld"], m["o_w"], m["o_st"]
        wbias, hot_zero = sem("wbias"), sem("hot_zero")
        o_bn, o_pow = ([sem(f"{n}{k}") for k in range(2)] for n in ("o_bn", "o_pow"))
        m["w1_ld"], m["w2_ld"], m["wbias"] = w1_ld, w2_ld, wbias

        pch, ch = Chain(nc.gpsimd, sem("p_chain1")), Chain(nc.vector, sem("v_chain5"))

        def sync_program(sp, tail):
            m["start"](sp)
            if tail:
                for h in range(2):
                    load_w1(sp, a, QB, h, m["w1_sb"][1], w1_ld[1])
                for h in range(2):
                    load_w2(sp, a, QB, h, m["w2_sb"][1], w2_ld[1])
                return
            sp.wait_ge(o_st, START + 16 * GROUPS)

            def load(i):
                sp.wait_ge(o_at, START + i)
                load_quad(sp, m, i)

            with nc.sync.Fori(1, 3) as i:
                load(i)
            load_bias(sp, a, m, wbias)
            for h in range(2):
                load_w1(sp, a, 0, h, m["w1_sb"][0], w1_ld[0])
            for h in range(2):
                load_w2(sp, a, 0, h, m["w2_sb"][0], w2_ld[0])
            with nc.sync.Fori(3, QUADS) as i:
                load(i)

        def scalar_head(act):
            act.wait_ge(o_gwt, START + 1)
            nc.scalar.copy(gw_t[:], ps_z[:, 0, 0:KT * X].rearrange("p (k x) -> p k x", k=KT)).then_inc(o_gwt_ok, 1)
            act.wait_ge(hot_zero, START + 1)

        def scalar_program(act, tail):
            def copy_x2(i):
                act.wait_ge(o_xt, START + i + 1)
                nc.scalar.copy(x2_t[:].rearrange("p j k c -> p (j k c)"), ps_z[:].rearrange("p j e -> p (j e)"))\
                    .then_inc(o_xtok, 1)

            def exponential(i):
                act.wait_ge(o_nm, START + i + 1)
                nc.scalar.activation(pr[:], lg[:], ACT.Exp, bias=nmx[:, 0:1], scale=1.0, accum_out=den[:, 0:1])\
                    .then_inc(o_ex, 1)

            def copy_picks(i):
                act.wait_ge(o_pt, START + i + 1)
                nc.scalar.copy(pm_t[:], ps_g[:, 1, 0:P]).then_inc(o_ptok, 1)

            def copy_merged(i):
                act.wait_ge(o_mm, START + i + 1)
                for k in range(KT):
                    ins = nc.scalar.copy(merged[:, k, :, bass.ds(QB * i, QB)],
                                         ps_g[:, 2, k * P:(k + 1) * P].rearrange("p (j x) -> p x j", j=QB))
                ins.then_inc(o_mc, 1)

            def copy_z(i):
                act.wait_ge(o_zt, START + i + 1)
                nc.scalar.copy(z_t[:].rearrange("p j k c -> p (j k c)"), ps_z[:].rearrange("p j e -> p (j e)"))\
                    .then_inc(o_ztok, 1)

            def copy_h2(i):
                for h in range(2):
                    act.wait_ge(o_h, START + 2 * i + h + 1)
                    nc.scalar.copy(h2[:, bass.ds(QB * i + 2 * h, 2)], ps_h[:, 2 * h:2 * h + 2]).then_inc(o_hc, 1)

            def gate_entries(i):
                act.wait_ge(o_gt, START + i)
                nc.scalar.copy(gq[:], g_tab[:, bass.ds(2 * i, 2)])

            def entries(i):
                act.wait_ge(o_h, START + 2 * i)
                for s in range(2):
                    rows = slice(s * C, (s + 1) * C)
                    last = nc.scalar.copy(hot[rows, s::2], onehot[rows, bass.ds(2 * i, 2)])
                last.then_inc(o_hot, 1)
                nc.scalar.copy(hq[:], h_tab[:, bass.ds(2 * i, 2)]).then_inc(o_hot, 1)

            def step(t, new=True, old=True, older=True):
                if older:
                    copy_x2(t - 2)
                if old:
                    copy_z(t - 1)
                if new:
                    gate_entries(t)
                if older:
                    exponential(t - 2)
                if old:
                    copy_h2(t - 1)
                if older:
                    copy_picks(t - 2)
                if new:
                    entries(t)
                if older:
                    copy_merged(t - 2)

            if tail:
                step(QUADS, new=False)
                step(QUADS + 1, new=False, old=False)
                return
            scalar_head(act)
            step(0, old=False, older=False)
            step(1, older=False)
            with nc.scalar.Fori(2, QUADS) as t:
                step(t)

        def gpsimd_program(pool, tail):

            def root(n, i):
                pool.wait_ge(o_bn[n], START + i + 1)
                nc.gpsimd.tensor_tensor(rs[:, n], ve[:, n], mhalf[:, 0:QB], ALU.pow).then_inc(o_pow[n], 1)

            def scale(i):
                pool.wait_ge(o_zn, START + i + 1)
                pch.link(nc.gpsimd.tensor_tensor(z[:], z[:], lng[:].unsqueeze(1).broadcast_to([P, QB, E]), ALU.mult))
                nc.gpsimd.tensor_tensor(z[:], z[:], lnb[:].unsqueeze(1).broadcast_to([P, QB, E]), ALU.add)\
                    .then_inc(o_zs, 1)

            def keep_picks(i):
                pool.wait_ge(o_pm, START + i + 1)
                nc.gpsimd.tensor_copy(picked[:, bass.ds(i, 1)], pm[:].unsqueeze(1)).then_inc(o_pmc, 1)

            def step(t, new=True, old=True, older=True):
                if new:
                    root(0, t)
                    scale(t)
                if old:
                    root(1, t - 1)
                if older:
                    keep_picks(t - 2)

            if tail:
                step(QUADS, new=False)
                step(QUADS + 1, new=False, old=False)
                return
            nc.gpsimd.memset(hot[:], 0.0).then_inc(hot_zero, 1)
            step(0, old=False, older=False)
            step(1, older=False)
            with nc.gpsimd.Fori(2, QUADS) as t:
                pch.enter(t, 1, 2)
                step(t)
            pch.leave(QUADS)

        def vector_program(dve, tail):
            def statistics(src, n, i):
                for j in range(QB):
                    if n == 1 and j % 2 == 0:
                        dve.wait_ge(o_hc, START + 2 * i + j // 2 + 1)
                    last = nc.vector.bn_stats(bn[:, j], src[:, j])
                ch.link(last)
                row_statistics(nc, ch, bn[:], mean[:, n], ve[:, n], tmp[:], EPS).then_inc(o_bn[n], 1)

            def input_statistics(i):
                dve.wait_ge(o_at, START + i + 1)
                statistics(ps_a, 0, i)

            def normalise(i):
                dve.wait_ge(o_pow[0], START + i + 1)
                dve.wait_ge(o_zt, START + i)
                for j in range(QB):
                    last = nc.vector.tensor_scalar(z[:, j], ps_a[:, j], mean[:, 0, j:j + 1], rs[:, 0, j:j + 1],
                                                   ALU.subtract, ALU.mult)
                last.then_inc(o_zn, 1)

            def gate(i):
                dve.wait_ge(o_gt, START + i + 1)
                dve.wait_ge(o_zs, START + i + 1)
                nc.vector.tensor_tensor(z[:], z[:], ps_g[:], ALU.mult).then_inc(o_z, 1)

            def normalise_h2(i):
                statistics(ps_h, 1, i)
                dve.wait_ge(o_pow[1], START + i + 1)
                dve.wait_ge(o_mm, START + i)
                for j in range(QB):
                    last = nc.vector.tensor_scalar(x2[:, j], ps_h[:, j], mean[:, 1, j:j + 1], rs[:, 1, j:j + 1],
                                                   ALU.subtract, ALU.mult)
                last.then_inc(o_x, 1)

            def softmax_input(i):
                dve.wait_ge(o_lg, START + i + 1)
                ch.link(nc.vector.tensor_scalar(lg[:], ps_g[:, 0, 0:T], gb[:, 0:1], None, ALU.add))
                nc.vector.tensor_reduce(nmx[:], lg[:], AX.X, ALU.max, negate=True).then_inc(o_nm, 1)

            def pick(i):
                dve.wait_ge(o_ex, START + i + 1)
                ch.link(nc.vector.reciprocal(rden[:], den[:]))
                ch.link(nc.vector.tensor_scalar(pr[:], pr[:], rden[:, 0:1], None, ALU.mult))
                nc.vector.tensor_copy(idle[:, 0:1], rden[:])
                ch.link(nc.vector.max(top8[:], pr[:]))
                nc.vector.tensor_copy(idle[:], top8[:])
                ch.link(nc.vector.match_replace(rep[:], top8[:], pr[:], -1.0))
                dve.wait_ge(o_pt, START + i)
                dve.wait_ge(o_pmc, START + i)
                nc.vector.scalar_tensor_tensor(pm[:], rep[:], 0.0, pr[:], ALU.is_lt, ALU.mult).then_inc(o_pm, 1)

            def step(t, new=True, old=True, older=True):
                if old:
                    gate(t - 1)
                if new:
                    input_statistics(t)
                if older:
                    softmax_input(t - 2)
                if new:
                    normalise(t)
                if older:
                    pick(t - 2)
                if old:
                    normalise_h2(t - 1)

            if tail:
                step(QUADS, new=False)
                step(QUADS + 1, new=False, old=False)
                return
            dve.wait_ge(o_w, START + 16 * 8)
            step(0, old=False, older=False)
            step(1, older=False)
            with nc.vector.Fori(2, QUADS) as t:
                ch.enter(t, 2 * 3 + 5, 2)
                step(t)
            ch.leave(QUADS)

        def tensor_head(pe):
            pe.wait_ge(o_w, START + 16 * 8)
            for k in range(KT):
                last = nc.tensor.transpose(ps_z[:, 0, k * X:(k + 1) * X], gw[:, k * P:(k + 1) * P], ident[0:X, 0:X])
            last.then_inc(o_gwt, 1)
            pe.wait_ge(o_gwt_ok, START + 1)

        def tensor_program(pe, tail):
            def transpose_in(i):
                pe.wait_ge(o_ld, START + 16 * i + 16)
                pe.wait_ge(o_zn, START + i)
                for j in range(QB):
                    for k in range(KT):
                        last = nc.tensor.transpose(ps_a[:, j, k * P:(k + 1) * P], ao[:, j, k], ident[:])
                last.then_inc(o_at, 1)

            def gates(i, older):
                pe.wait_ge(o_hot, START + 2 * i + 1)
                pe.wait_ge(o_z, START + i)
                pe.wait_ge(o_mc, START + older)
                for j in range(QB):
                    last = nc.tensor.matmul(ps_g[:, j], hot[:, j], gq[:, j // 2], start=True, stop=True)
                last.then_inc(o_gt, 1)

            def transpose_z(i, older):
                pe.wait_ge(o_z, START + i + 1)
                pe.wait_ge(o_xtok, START + older)
                for j in range(QB):
                    for k in range(KT):
                        last = nc.tensor.transpose(ps_z[:, j, k * P:(k + 1) * P], z[:, j, k * P:(k + 1) * P], ident[:])
                last.then_inc(o_zt, 1)

            def residual_and_project(i):
                pe.wait_ge(o_ztok, START + i + 1)
                pe.wait_ge(o_hot, START + 2 * i + 2)
                pe.wait_ge(o_x, START + i)
                for j in range(QB):
                    nc.tensor.matmul(ps_h[:, j], hot[:, j], hq[:, j // 2], start=True, stop=False)
                    for k in range(KT):
                        last = nc.tensor.matmul(ps_h[:, j], z_t[:, j, k], w_out[:, k], start=False, stop=k == KT - 1)
                    if j % 2:
                        last.then_inc(o_h, 1)

            def transpose_x2(i):
                pe.wait_ge(o_x, START + i + 1)
                pe.wait_ge(o_ztok, START + i + 1)
                for j in range(QB):
                    for k in range(KT):
                        last = nc.tensor.transpose(ps_z[:, j, k * P:(k + 1) * P], x2[:, j, k * P:(k + 1) * P], ident[:])
                last.then_inc(o_xt, 1)

            def logits(i):
                pe.wait_ge(o_xtok, START + i + 1)
                for j in range(QB):
                    for k in range(KT):
                        last = nc.tensor.matmul(ps_g[j * X:(j + 1) * X, 0, 0:T], gw_t[:, k], x2_t[:, j, k],
                                                start=k == 0, stop=k == KT - 1)
                last.then_inc(o_lg, 1)

            def merge(i):
                pe.wait_ge(o_pm, START + i + 1)
                nc.tensor.transpose(ps_g[:, 1, 0:P], pm[:], ident[:]).then_inc(o_pt, 1)
                pe.wait_ge(o_ptok, START + i + 1)
                for j in range(QB):
                    for k in range(KT):
                        last = nc.tensor.matmul(ps_g[:, 2, k * P + j * X:k * P + (j + 1) * X],
                                                x2[:, j].rearrange("t (p k) -> t k p", k=KT)[:, k],
                                                pm_t[:, j * X:(j + 1) * X], start=True, stop=True)
                last.then_inc(o_mm, 1)

            def step(t, new=True, old=True, older=True):
                if older:
                    transpose_x2(t - 2)
                if new:
                    transpose_in(t)
                if old:
                    transpose_z(t - 1, t - 1 if older else 0)
                if older:
                    logits(t - 2)
                if old:
                    residual_and_project(t - 1)
                if older:
                    merge(t - 2)
                if new:
                    gates(t, t - 1 if older else 0)

            if tail:
                step(QUADS, new=False)
                step(QUADS + 1, new=False, old=False)
                return
            tensor_head(pe)
            step(0, old=False, older=False)
            step(1, older=False)
            with nc.tensor.Fori(2, QUADS) as t:
                step(t)

        for tail in (False, True):
            if tail:
                replace_tables()
            with nc.Block() as block:
                @block.sync
                def _(sp):
                    sync_program(sp, tail)

                @block.scalar
                def _(act):
                    scalar_program(act, tail)

                @block.gpsimd
                def _(pool):
                    gpsimd_program(pool, tail)

                @block.vector
                def _(dve):
                    vector_program(dve, tail)

                @block.tensor
                def _(pe):
                    tensor_program(pe, tail)


def load_bias(eng, a, m, done):
    eng.dma_start(m["b1_sb"][:], a["L0_ffn_w1"][:, E]).then_inc(done, 16)
    eng.dma_start(m["b2_sb"][:], a["L0_ffn_w2"][:, HID]).then_inc(done, 16)


def load_w1(eng, a, x, h, dst, done):
    eng.dma_start(dst[:, :, h],
                  a["L0_ffn_w1"][bass.ds(x, QB), 0:E].rearrange("x (p k) n -> k p x n", k=KT)[h]).then_inc(done[h], 16)


def load_w2(eng, a, x, h, dst, done):
    half = slice(h * HT // 2, (h + 1) * HT // 2)
    eng.dma_start(dst[:, :, half].rearrange("p x n e -> p x (n e)"),
                  a["L0_ffn_w2"][bass.ds(x, QB), 0:HID].rearrange("x (p h n) e -> h p x (n e)", h=2, n=HT // 2)[h])\
        .then_inc(done[h], 16)


def experts(nc, a, m, sem, sb):
    ident, merged, exp_out = m["ident"], m["merged"], m["exp_out"]
    w1, w2, b1, b2, w1_ld, w2_ld = m["w1_sb"], m["w2_sb"], m["b1_sb"], m["b2_sb"], m["w1_ld"], m["w2_ld"]
    mq = [sb(f"mq{s}", [P, KT, QB, B]) for s in range(2)]
    sel = [sb(f"sel{s}", [X, QB, B]) for s in range(2)]
    hg = sb("hg", [P, HID])
    h_t = sb("h_t", [P, HT, P])
    eo = sb("eo", [P, X // QB, E])

    with ExitStack() as ctx:
        ps_1 = [ctx.enter_context(nc.psum_tensor(f"ps_1{s}", [P, HID], F32)) for s in range(2)]
        ps_t = ctx.enter_context(nc.psum_tensor("ps_ht", [P, HT, P], F32))
        ps_2 = [ctx.enter_context(nc.psum_tensor(f"ps_2{s}", [P, 512], F32)) for s in range(2)]
        block = ctx.enter_context(nc.Block())
        mq_ok, gl, ht, htok, eo_ok, eo_st = (
            sem(n) for n in ("mq_ok", "gl", "ht", "htok", "eo_ok", "eo_st"))
        l1, l2 = ([sem(f"{n}{s}") for s in range(2)] for n in ("l1_", "l2_"))
        TURNS = X // QB // 2


        @block.scalar
        def _(act):
            def operands(i, s):
                q = 2 * i + s
                act.wait_ge(l2[s], START + 2 * i)
                nc.scalar.copy(mq[s][:], merged[:, :, bass.ds(QB * q, QB)])
                nc.scalar.copy(sel[s][:], ident[0:X, bass.ds(QB * q, QB)].unsqueeze(2)
                               .broadcast_to([X, QB, B])).then_inc(mq_ok, 1)

            def hidden(i, s):
                act.wait_ge(l1[s], START + 2 * i + 2)
                act.wait_ge(ht, START + 4 * i + 2 * s)
                nc.scalar.activation(hg[:], ps_1[s][:], ACT.Gelu).then_inc(gl, 1)

            operands(0, 0)
            operands(0, 1)
            with nc.scalar.Fori(0, TURNS - 1) as i:
                for s in range(2):
                    hidden(i, s)
                    operands(i + 1, s)
            for s in range(2):
                hidden(TURNS - 1, s)

        @block.sync
        def _(sp):
            m["start"](sp)

            def store(q):
                sp.wait_ge(eo_ok, START + q + 1)
                sp.dma_start(exp_out[:, bass.ds(QB * q, QB)].rearrange("b x e -> x b e"),
                             eo[:, bass.ds(q, 1)].rearrange("p i e -> p (i e)")).then_inc(eo_st, 16)

            def first_weights(i, s):
                for h in range(2):
                    sp.wait_ge(l1[s], START + 2 * i - 1 + h)
                    load_w1(sp, a, QB * (2 * i + s), h, w1[s], w1_ld[s])

            def second_weights(i, s):
                for h in range(2):
                    sp.wait_ge(l2[s], START + 2 * i - 1 + h)
                    load_w2(sp, a, QB * (2 * i + s), h, w2[s], w2_ld[s])
                store(2 * (i - 1) + s)

            first_weights(1, 0)
            with nc.sync.Fori(1, TURNS - 1) as i:
                first_weights(i, 1)
                second_weights(i, 0)
                first_weights(i + 1, 0)
                second_weights(i, 1)
            first_weights(TURNS - 1, 1)
            for s in range(2):
                second_weights(TURNS - 1, s)
            for s in range(2):
                store(2 * (TURNS - 1) + s)
            sp.wait_ge(eo_st, START + 16 * TURNS * 2)

        @block.vector
        def _(dve):
            with nc.vector.Fori(0, TURNS) as i:
                for s in range(2):
                    dve.wait_ge(l2[1 - s], START + 2 * i + 2 * s)
                    for h in range(2):
                        dve.wait_ge(ht, START + 4 * i + 2 * s + h + 1)
                        half = slice(h * HT // 2, (h + 1) * HT // 2)
                        nc.vector.tensor_copy(h_t[:, half], ps_t[:, half]).then_inc(htok, 1)
                    dve.wait_ge(l2[s], START + 2 * i + 2)
                    nc.vector.tensor_copy(eo[:, bass.ds(2 * i + s, 1)], ps_2[s][:, 0:E].unsqueeze(1)).then_inc(eo_ok, 1)

        @block.tensor
        def _(pe):
            def first_layer(i, s):
                pe.wait_ge(mq_ok, START + 2 * i + s + 1)
                pe.wait_ge(gl, START + 2 * i + s - 1)
                for n in range(2):
                    cols = slice(n * 512, (n + 1) * 512)
                    nc.tensor.matmul(ps_1[s][:, cols], sel[s][:].rearrange("x j b -> x (j b)"), b1[:, cols],
                                     start=True, stop=False, skip_group_check=True)
                for k in range(KT):
                    pe.wait_ge(w1_ld[s][k], START + 16 * i + 16)
                    for n in range(2):
                        cols = slice(n * 512, (n + 1) * 512)
                        for j in range(QB):
                            last = nc.tensor.matmul(ps_1[s][j * B:(j + 1) * B, cols], mq[s][:, k, j],
                                                    w1[s][:, j, k, cols], start=False, stop=k == KT - 1,
                                                    skip_group_check=True)
                    last.then_inc(l1[s], 1)

            def transpose_hidden(i, s):
                pe.wait_ge(gl, START + 2 * i + s + 1)
                pe.wait_ge(htok, START + 4 * i + 2 * s)
                for h in range(2):
                    for n in range(h * HT // 2, (h + 1) * HT // 2):
                        last = nc.tensor.transpose(ps_t[:, n], hg[:].rearrange("q (p n) -> q n p", n=HT)[:, n], ident[:])
                    last.then_inc(ht, 1)

            def second_layer(i, s):
                pe.wait_ge(eo_ok, START + 2 * i + s)
                nc.tensor.matmul(ps_2[s][:, 0:E], sel[s][:].rearrange("x j b -> x (j b)"), b2[:],
                                 start=True, stop=False, skip_group_check=True)
                for n in range(HT):
                    if n % (HT // 2) == 0:
                        pe.wait_ge(w2_ld[s][n // (HT // 2)], START + 16 * i + 16)
                        pe.wait_ge(htok, START + 4 * i + 2 * s + n // (HT // 2) + 1)
                    for j in range(QB):
                        last = nc.tensor.matmul(ps_2[s][j * B:(j + 1) * B, 0:E], h_t[:, n, j * B:(j + 1) * B],
                                                w2[s][:, j, n], start=False, stop=n == HT - 1, skip_group_check=True)
                    if n % (HT // 2) == HT // 2 - 1:
                        last.then_inc(l2[s], 1)

            pe.wait_ge(m["wbias"], START + 32)
            first_layer(0, 0)
            first_layer(0, 1)
            transpose_hidden(0, 0)
            second_layer(0, 0)
            with nc.tensor.Fori(1, TURNS) as i:
                first_layer(i, 0)
                transpose_hidden(i - 1, 1)
                second_layer(i - 1, 1)
                first_layer(i, 1)
                transpose_hidden(i, 0)
                second_layer(i, 0)
            transpose_hidden(TURNS - 1, 1)
            second_layer(TURNS - 1, 1)


def combine(nc, m, sem, out):
    h2, picked, exp_out = m["h2"], m["picked"], m["exp_out"]
    with ExitStack() as ctx:
        def sbx(n, s):
            return ctx.enter_context(nc.sbuf_tensor(n, s, F32))
        oq = sbx("oq", [P, QUADS, E])
        res = [sbx(f"res{s}", [P, QB, E]) for s in range(2)]
        ps_o = [ctx.enter_context(nc.psum_tensor(f"ps_fo{j}", [P, 512], F32)) for j in range(QB)]
        ps_o2 = [ctx.enter_context(nc.psum_tensor(f"ps_go{j}", [P, 512], F32)) for j in range(QB)]
        psx = [ps_o, ps_o2]
        block = ctx.enter_context(nc.Block())

        def par(name):
            return [sem(f"{name}{i}") for i in range(2)]
        f_mm, f_add, f_out = (par(n) for n in ("z_mm", "z_add", "z_out"))
        f_ld = sem("z_ld")
        TURNS = QUADS // 2

        @block.sync
        def _(sp):
            m["start"](sp)
            src = exp_out.rearrange("(q j) x e -> (j x) q e", j=QB)
            for h in range(2):
                quads = slice(h * QUADS // 2, (h + 1) * QUADS // 2)
                sp.dma_start(oq[:, quads], src[:, quads]).then_inc(f_ld, 16)
                sp.wait_ge(f_ld, START + 16 * (h + 1))

        @block.tensor
        def _(pe):
            for q in range(QUADS):
                i, s = divmod(q, 2)
                if q % (QUADS // 2) == 0:
                    pe.wait_ge(f_ld, START + (32 if q else 16))
                pe.wait_ge(f_add[s], START + i)
                for j in range(QB):
                    rows = slice(j * X, (j + 1) * X)
                    last = nc.tensor.matmul(psx[s][j][:, 0:E], picked[rows, q], oq[rows, q], start=True, stop=True)
                last.then_inc(f_mm[s], 1)

        @block.vector
        def _(dve):
            with nc.vector.Fori(0, TURNS) as i:
                for s in range(2):
                    dve.wait_ge(f_mm[s], START + i + 1)
                    dve.wait_ge(f_out[s], START + 16 * i)
                    for j in range(QB):
                        last = nc.vector.tensor_tensor(res[s][:, bass.ds(j, 1)], psx[s][j][:, 0:E].unsqueeze(1),
                                                       h2[:, bass.ds(2 * QB * i + QB * s + j, 1)], ALU.add)
                    last.then_inc(f_add[s], 1)

        @block.scalar
        def _(act):
            dst = out.rearrange("(q j) t e -> q t j e", j=QB)
            with nc.scalar.Fori(0, TURNS) as i:
                for s in range(2):
                    act.wait_ge(f_add[s], START + i + 1)
                    act.dma_start(dst[bass.ds(2 * i + s, 1)].rearrange("q t j e -> (q t) j e"), res[s][:])\
                        .then_inc(f_out[s], 16)
            for s in range(2):
                act.wait_ge(f_out[s], START + 16 * TURNS)


_INS = ["x", "L0_tok_emb_W", "L0_tok_emb_b", "L0_tok_Wq", "L0_tok_bq", "L0_tok_Wk", "L0_tok_bk", "L0_tok_Wv",
        "L0_tok_bv", "L0_tok_Wo", "L0_tok_bo", "L0_attn_Wq", "L0_attn_Wk", "L0_attn_Wv", "L0_attn_Wbeta",
        "L0_attn_Wg", "L0_attn_Wout", "L0_attn_ln_g", "L0_attn_ln_b", "L0_ffn_gate_w", "L0_ffn_gate_b",
        "L0_ffn_w1", "L0_ffn_w2"]


def kernel(**inputs):
    import numpy as _np
    import concourse.bacc as _bacc
    from concourse import mybir as _mybir
    from concourse.bass_utils import run_bass_kernel_spmd as _run

    nc = _bacc.Bacc("TRN2", target_bir_lowering=False, num_devices=1)
    arrays, args = {}, {}
    for name in _INS:
        v = _np.ascontiguousarray(inputs[name])
        arrays[f"in_{name}"] = v
        args[name] = nc.dram_tensor(f"in_{name}", v.shape, _mybir.dt.from_np(v.dtype), kind="ExternalInput").ap()
    out = nc.dram_tensor("out_dram", (B, T, E), _mybir.dt.float32, kind="ExternalOutput").ap()
    tower(nc, args, out)
    r = _run(nc, [arrays], core_ids=[0])
    return r.results[0]["out_dram"]
```
